# Optimizing a Trainium2 kernel written in Bass

```python
import numpy as np
import jax
import jax.numpy as jnp

def _softmax(x, axis=-1):
    return jax.nn.softmax(x, axis=axis)

def _gelu(x):
    return jax.nn.gelu(x, approximate=True)

def _silu(x):
    return jax.nn.silu(x)

def _sigmoid(x):
    return jax.nn.sigmoid(x)

def _layernorm(x, axis=-1, eps=1e-05):
    m = jnp.mean(x, axis=axis, keepdims=True)
    v = jnp.var(x, axis=axis, keepdims=True)
    return (x - m) / jnp.sqrt(v + eps)

def _scatter_add(tgt, idx, src, axis=0):
    return tgt.at[idx].add(src)

def _segment_sum(src, seg, n):
    return jax.ops.segment_sum(src, seg, n)
kernel_name = 'mk_flamingo_gated_d1_seqx_r4_a6f72b'

def setup_inputs(seed: int=0):
    np.random.seed(seed)
    _w = jnp.asarray

    def _rec_inputs():
        import jax
        import jax.numpy as jnp
        _rk = jax.random.key(seed)
        x = -7.109e-05 + 0.9999 * jax.random.normal(jax.random.fold_in(_rk, 1), (4, 512, 512), jnp.float32)
        _lenS = 512 - jax.random.randint(jax.random.fold_in(_rk, 7), (4,), 0, max(1, 512 // 4) + 1, jnp.int32)
        _lenS2 = 512 - jax.random.randint(jax.random.fold_in(_rk, 8), (4,), 0, max(1, 512 // 4) + 1, jnp.int32)
        _ctx_512P = jax.random.normal(jax.random.fold_in(_rk, 11), (4, 16, 128), jnp.float32)
        _ctx_512c = jax.random.dirichlet(jax.random.fold_in(_rk, 511), 0.3 * jnp.ones((16,), jnp.float32), (4, 512))
        _ctx_512t = jnp.einsum('bsk,bkd->bsd', _ctx_512c, _ctx_512P)
        _ctx_512t = _ctx_512t * jax.lax.rsqrt(jnp.mean(jnp.square(_ctx_512t)) + 1e-12) * 0.953939
        ctx_512 = 2.81802e-05 + 1.00001 * (_ctx_512t + 0.3 * jax.random.normal(jax.random.fold_in(_rk, 611), (4, 512, 128), jnp.float32))
        _g = jax.random.normal(jax.random.fold_in(_rk, 9001), (2, 1), jnp.float32)
        _g = jnp.sign(_g) * jnp.maximum(jnp.abs(_g), 1.0) + (_g == 0) * 1.0
        g_xattn = _g[0]
        g_ffn = _g[1]
        return (x, ctx_512, g_xattn, g_ffn)
    x, ctx_512, g_xattn, g_ffn = _rec_inputs()

    def _L0_xattn_setup():
        import jax, jax.numpy as jnp
        import numpy as np
        EPS = 1e-06
        IMAGE_DIMS = 512
        key = jax.random.key(seed)
        k1, k2, k3 = jax.random.split(key, 3)
        B, I, J, D = (16, 512, 512, 128)
        p = jax.random.normal(k1, (B, I, J), dtype=jnp.float32)
        k_v = jax.random.normal(k2, (B, J, D), dtype=jnp.float32)
        W_k = jax.random.normal(k3, (D, D), dtype=jnp.float32) * (1.0 / np.sqrt(D))
        b_k = jnp.zeros((D,), dtype=jnp.float32)
        ln_gamma = jnp.ones((J,), dtype=jnp.float32)
        ln_beta = jnp.zeros((J,), dtype=jnp.float32)
        return {'p': p, 'k_v': k_v, 'W_k': W_k, 'b_k': b_k, 'ln_gamma': ln_gamma, 'ln_beta': ln_beta}
    _L0_xattn_all = _L0_xattn_setup()
    _L0_xattn_in = {k: v for k, v in _L0_xattn_all.items() if k in ('W_k', 'b_k', 'ln_gamma', 'ln_beta')}
    del _L0_xattn_all

    def _L0_ffn_setup():
        import jax, jax.numpy as jnp
        import numpy as np
        B, S, H = (2, 256, 512)
        E, K, F = (8, 2, 352)
        N_SHARED = 2
        FS = F * N_SHARED
        ROUTED_SCALE = 1.0

        def _swiglu_mlp(x, wg, wu, wd):
            return jax.nn.silu(x @ wg.T) * (x @ wu.T) @ wd.T
        key = jax.random.key(seed)
        ks = jax.random.split(key, 8)

        def w(k, shape, fan_in):
            return jax.random.normal(k, shape, jnp.float32) * (1.0 / np.sqrt(fan_in))
        return {'hidden_states': jax.random.normal(ks[0], (B, S, H), jnp.float32), 'gate_weight': w(ks[1], (E, H), H), 'w_gate': w(ks[2], (E, F, H), H), 'w_up': w(ks[3], (E, F, H), H), 'w_down': w(ks[4], (E, H, F), F), 'sw_gate': w(ks[5], (FS, H), H), 'sw_up': w(ks[6], (FS, H), H), 'sw_down': w(ks[7], (H, FS), FS)}
    _L0_ffn_all = _L0_ffn_setup()
    _L0_ffn_in = {k: v for k, v in _L0_ffn_all.items() if k in ('gate_weight', 'w_gate', 'w_up', 'w_down', 'sw_gate', 'sw_up', 'sw_down')}
    del _L0_ffn_all
    return {'x': x, 'ctx_512': ctx_512, 'g_xattn': g_xattn, 'g_ffn': g_ffn, 'L0_xattn_W_k': _L0_xattn_in['W_k'], 'L0_xattn_b_k': _L0_xattn_in['b_k'], 'L0_xattn_ln_gamma': _L0_xattn_in['ln_gamma'], 'L0_xattn_ln_beta': _L0_xattn_in['ln_beta'], 'L0_ffn_gate_weight': _L0_ffn_in['gate_weight'], 'L0_ffn_w_gate': _L0_ffn_in['w_gate'], 'L0_ffn_w_up': _L0_ffn_in['w_up'], 'L0_ffn_w_down': _L0_ffn_in['w_down'], 'L0_ffn_sw_gate': _L0_ffn_in['sw_gate'], 'L0_ffn_sw_up': _L0_ffn_in['sw_up'], 'L0_ffn_sw_down': _L0_ffn_in['sw_down']}

def reference(x, ctx_512, g_xattn, g_ffn, L0_xattn_W_k, L0_xattn_b_k, L0_xattn_ln_gamma, L0_xattn_ln_beta, L0_ffn_gate_weight, L0_ffn_w_gate, L0_ffn_w_up, L0_ffn_w_down, L0_ffn_sw_gate, L0_ffn_sw_up, L0_ffn_sw_down):
    import jax
    import jax.numpy as jnp

    def _L0_xattn_ref(p, k_v, W_k, b_k, ln_gamma, ln_beta):
        import jax, jax.numpy as jnp
        import numpy as np
        EPS = 1e-06
        IMAGE_DIMS = 512
        kv = k_v @ W_k.T + b_k
        out = jnp.einsum('bij,bjd->bid', p, kv)
        scale = IMAGE_DIMS ** (-0.5)
        sim = jnp.einsum('bid,bjd->bij', out, kv) * scale
        mu = jnp.mean(sim, axis=-1, keepdims=True)
        var = jnp.var(sim, axis=-1, keepdims=True)
        sim = (sim - mu) * jax.lax.rsqrt(var + EPS) * ln_gamma + ln_beta
        attn = jax.nn.softmax(sim, axis=-1)
        return attn

    def _L0_ffn_ref(hidden_states, gate_weight, w_gate, w_up, w_down, sw_gate, sw_up, sw_down):
        import jax, jax.numpy as jnp
        import numpy as np
        B, S, H = (2, 256, 512)
        E, K, F = (8, 2, 352)
        N_SHARED = 2
        FS = F * N_SHARED
        ROUTED_SCALE = 1.0

        def _swiglu_mlp(x, wg, wu, wd):
            return jax.nn.silu(x @ wg.T) * (x @ wu.T) @ wd.T
        b, s, h = hidden_states.shape
        x = hidden_states.reshape(-1, h)
        T = x.shape[0]
        logits = x.astype(jnp.float32) @ gate_weight.astype(jnp.float32).T
        scores = jax.nn.softmax(logits, axis=-1)
        topk_w, topk_idx = jax.lax.top_k(scores, K)
        topk_w = topk_w / (jnp.sum(topk_w, axis=-1, keepdims=True) + 1e-20)
        topk_w = topk_w * ROUTED_SCALE
        cw = jnp.zeros((T, E), jnp.float32).at[jnp.arange(T)[:, None], topk_idx].add(topk_w)
        g = jax.nn.silu(jnp.einsum('th,efh->tef', x, w_gate)) * jnp.einsum('th,efh->tef', x, w_up)
        expert_out = jnp.einsum('tef,ehf->teh', g, w_down)
        y = jnp.einsum('te,teh->th', cw, expert_out).reshape(b, s, h)
        y = y + _swiglu_mlp(x, sw_gate, sw_up, sw_down).reshape(b, s, h)
        return y
    x = x + jnp.tanh(g_xattn[0]) * _L0_xattn_ref(_layernorm(x, axis=-1), ctx_512, L0_xattn_W_k, L0_xattn_b_k, L0_xattn_ln_gamma, L0_xattn_ln_beta)
    x = x + jnp.tanh(g_ffn[0]) * _L0_ffn_ref(_layernorm(x, axis=-1), L0_ffn_gate_weight, L0_ffn_w_gate, L0_ffn_w_up, L0_ffn_w_down, L0_ffn_sw_gate, L0_ffn_sw_up, L0_ffn_sw_down)
    return x

_drawn_inputs = setup_inputs


def setup_inputs(seed=0):
    import zlib

    import numpy as np

    out = dict(_drawn_inputs(seed))
    spreads = {'L0_xattn_b_k': (0.0, 2.0),
     'L0_xattn_ln_gamma': (1.0, 0.6),
     'L0_xattn_ln_beta': (0.0, 2.0)}
    factors = {'ctx_512': 3.975, 'L0_xattn_W_k': 8.0}
    for name, (base, spread) in spreads.items():
        noise = np.random.default_rng([zlib.crc32(name.encode()), seed]).standard_normal(out[name].shape)
        drawn = base * np.exp(spread * noise) if base else spread * noise
        out[name] = jnp.asarray(drawn.astype(out[name].dtype))
    for name, factor in factors.items():
        out[name] = (out[name] * factor).astype(out[name].dtype)
    return out
```

```python
import concourse.bass as bass
from concourse import mybir
from contextlib import ExitStack

B, I, H = 4, 512, 512
DC = 128
E, F, TOPK = 8, 352, 2
P = 128
T = B * I
NTILE = T // P
NPAIR = NTILE // 2
HC = H // P
FC = -(-F // P)
FP = FC * P
GATE, UP, DOWN = 0, HC * F, 2 * HC * F
UNIT = DOWN + FC * H
QUARTERS = 4
CHUNK = UNIT // QUARTERS
SHARED_UNITS = 2
NCHUNK = (SHARED_UNITS + E) * QUARTERS
SLOT_TILES = (T * TOPK + E * (P - 1)) // P
AHEAD = 2
TABLE = SLOT_TILES + AHEAD
META_ROWS = E * T + 10 * P
LN_EPS, SIM_EPS = 1e-5, 1e-6
WSCALE = 256.0


def flamingo_block(nc, x, xT, ctxT, wkT, bk, gates, gamma, beta, gwT, wsrc, out):
    fp32, fp16 = mybir.dt.float32, mybir.dt.float16
    i32, u32 = mybir.dt.int32, mybir.dt.uint32
    ALU, ACT, AX = mybir.AluOpType, mybir.ActivationFunctionType, mybir.AxisListType
    ds = bass.ds

    x1_d = nc.dram_tensor("x1_d", (T, H), fp32, kind="Internal").ap()
    hid_d = nc.dram_tensor("hid_d", (T + P, 2 * H), fp16, kind="Internal").ap()
    meta_d = nc.dram_tensor("meta_d", (META_ROWS, 2), i32, kind="Internal").ap()

    def by_tile(ap):
        return ap[0:T, :].rearrange("(n p) d -> n p d", p=P)

    x_pairs = x.rearrange("(n t p) d -> n p t d", t=2, p=P)
    x1_tiles, hid_tiles, out_tiles = by_tile(x1_d), by_tile(hid_d), by_tile(out)

    ctx = ExitStack()
    with ctx:
        def sb(name, shape, dt):
            return ctx.enter_context(nc.sbuf_tensor(name, shape, dt))

        def pb(name, shape, dt):
            return ctx.enter_context(nc.psum_tensor(name, shape, dt))

        def sem(name):
            return ctx.enter_context(nc.semaphore(name))

        ws = sb("ws", [P, SHARED_UNITS, 2, UNIT], fp16)
        wr = sb("wr", [P, E, 2, UNIT], fp16)

        def overlay(expert, offset, words, dt=fp32):
            flat = wr[:, :, :, :].rearrange("p e s n -> p (e s n)")
            at = expert * 2 * UNIT + 2 * offset
            v = flat[:, at:at + 2 * words]
            return v if dt == fp16 else v.bitcast(dt)

        ctx_t = overlay(3, 0, B * I).rearrange("p (b i) -> p b i", b=B)
        x_t = overlay(4, 0, B * HC * I).rearrange("p (b c i) -> p b c i", b=B, c=HC)
        kvc = overlay(4, B * HC * I, HC * DC).rearrange("p (c d) -> p c d", c=HC)
        kvc_t = overlay(6, 0, B * I).rearrange("p (b i) -> p b i", b=B)
        out_t = overlay(6, B * I, B * I).rearrange("p (b i) -> p b i", b=B)
        xb = overlay(6, 2 * B * I, 4 * H).rearrange("p (r t d) -> p r t d", r=2, t=2)
        nb = overlay(6, 2 * B * I + 4 * H, 2 * H).rearrange("p (t d) -> p t d", t=2)
        gamma_b = overlay(6, 2 * B * I + 6 * H, H)
        beta_b = overlay(6, 2 * B * I + 7 * H, H)
        hl0 = overlay(6, 2 * B * I + 8 * H, H, fp16).rearrange("p (s d) -> p s d", s=2)

        stage = sb("stage", [P, 2, CHUNK], fp32)
        ring = sb("ring", [P, 2, 2, 2, HC, P], fp16)
        xg_t = sb("xg_t", [P, 2, 2, HC, P], fp16)
        hl1 = xg_t[:, 1, :, :, :].rearrange("p s c n -> p s (c n)")
        outs = xg_t[:, 0, :, :, :].rearrange("p s c n -> p (s c n)").bitcast(fp32)[:, 0:2 * P]\
            .rearrange("p (t i) -> p t i", t=2)
        act_h = sb("act_h", [P, 2, F], fp32)
        act_hl = sb("act_hl", [P, 2, 2, FP], fp16)
        act_t = sb("act_t", [P, 2, 2, FC, P], fp16)
        yb = sb("yb", [P, 2, H], fp32)
        gath = ring[:, 0, :, :, :, :].rearrange("p t s c n -> p t s (c n)")
        hl = [hl0, hl1]

        id32 = overlay(3, B * I + 1536, P)
        id16 = sb("id16", [P, P], fp16)
        below = sb("below", [P, P], fp16)
        ones = sb("ones", [P, P], fp16)
        wk_sb = overlay(3, B * I + 1536 + P, DC)
        bk_sb = sb("bk_sb", [P, 1], fp32)
        ksum = sb("ksum", [P, B], fp32)
        kmean = sb("kmean", [P, B], fp32)
        g_sb = sb("g_sb", [P, 2], fp32)
        tg = sb("tg", [P, 2], fp32)
        tgs = sb("tgs", [P, 1], fp32)
        gw = overlay(3, B * I + 1536 + 2 * P, HC * E).rearrange("p (c e) -> p c e", c=HC)
        gwhl = sb("gwhl", [P, 2, HC, E], fp16)
        half_m = sb("half_m", [P, 2], fp32)
        stx = sb("stx", [P, 2, 6], fp32)
        sts = sb("sts", [P, 2, 6], fp32)
        st1 = sb("st1", [P, 2, 6], fp32)
        mvx = sb("mvx", [P, 2, 2], fp32)
        mvs = sb("mvs", [P, 2, 2], fp32)
        mv1 = sb("mv1", [P, 2, 2], fp32)
        q1a = sb("q1a", [P, 2], fp32)
        q1 = sb("q1", [P, 2], fp32)
        r1 = sb("r1", [P, 2], fp32)
        q2 = sb("q2", [P, 2], fp32)
        r2 = sb("r2", [P, 2], fp32)
        nmr = sb("nmr", [P, 2], fp32)
        top = sb("top", [P, 2], fp32)
        ntop = sb("ntop", [P, 2], fp32)
        esum = sb("esum", [P, 2], fp32)
        rsum = sb("rsum", [P, 2], fp32)
        coef = sb("coef", [P, 2], fp32)
        lg = sb("lg", [P, 2, E], fp32)
        s8 = sb("s8", [P, 2, 8], fp32)
        i8 = sb("i8", [P, 2, 8], u32)
        idxf = sb("idxf", [P, 2, 2], fp32)
        iota8 = sb("iota8", [P, 2, E], fp32)
        mask = sb("mask", [P, 2, 2, E], fp32)
        both = sb("both", [P, 2, E], fp16)
        before = sb("before", [P, 3, E], fp16)
        nl = sb("nl", [P, 2], fp32)
        es = sb("es", [P, 2, 8], fp32)
        ez = sb("ez", [P, 2], fp32)
        rz = sb("rz", [P, 2], fp32)
        p12 = sb("p12", [P, 2, 2], fp32)
        psm = sb("psm", [P, 2], fp32)
        pse = sb("pse", [P, 2], fp32)
        prs = sb("prs", [P, 2], fp32)
        first_slot = sb("first_slot", [P, 2, E], fp32)
        rk = sb("rk", [P, 2, E], fp32)
        rkm = sb("rkm", [P, 2, 2, E], fp32)
        slf = sb("slf", [P, 2, 2], fp32)
        sli = sb("sli", [P, 2, 2], i32)
        tok = sb("tok", [P, 2], fp32)
        mt = sb("mt", [P, 2, 2, 2], i32)
        fill = overlay(3, B * I, 2 * (META_ROWS // P), i32).rearrange("p (c k) -> p c k", k=2)
        filla = overlay(3, B * I + 512, META_ROWS // P, i32)
        zero = overlay(3, B * I + 1024, H, fp32)
        meta = sb("meta", [P, TABLE, 2], i32)
        idxg = sb("idxg", [P, 2], i32)
        idxs = sb("idxs", [P, 2], i32)
        cnt = sb("cnt", [1, 2, E], i32)
        tiles = sb("tiles", [1, E], fp32)
        ends = sb("ends", [1, 4, E], fp32)
        iota_s = sb("iota_s", [1, TABLE], fp32)
        tab = sb("tab", [1, 3, TABLE], fp32)
        te = sb("te", [1, TABLE], i32)
        tr = sb("tr", [1, TABLE], i32)

        misc = pb("misc", [P, 512], fp32)
        sim_ps = pb("sim_ps", [P, 2, 512], fp32)
        g_ps = pb("g_ps", [P, 512], fp32)
        u_ps = pb("u_ps", [P, 512], fp32)
        d_ps = pb("d_ps", [P, 512], fp32)
        xt_ps = pb("xt_ps", [P, 2, HC, P], fp16)
        ht_ps = pb("ht_ps", [P, 1024], fp16)
        ht_v = ht_ps[:, 0:2 * FP].rearrange("p (s c n) -> p s c n", s=2, c=FC)
        lg_ps = misc[:, 0:2 * E]
        rk_ps = misc[:, 32:32 + 2 * E]
        tot_ps = misc[:, 64:64 + E]

        d_ctx, d_small, d_gw = sem("d_ctx"), sem("d_small"), sem("d_gw")
        d_xt = [sem(f"d_xt{b}") for b in range(B)]
        d_x = [sem(f"d_x{r}") for r in range(2)]
        d_st = [sem(f"d_st{r}") for r in range(2)]
        d_x1w = [sem(f"d_x1w{t}") for t in range(2)]
        d_x1r = [sem(f"d_x1r{t}") for t in range(2)]
        d_hid = [sem(f"d_hid{t}") for t in range(2)]
        d_out = [sem(f"d_out{t}") for t in range(2)]
        d_fill, d_slots, d_add = sem("d_fill"), sem("d_slots"), sem("d_add")
        d_meta = [sem(f"d_meta{r}") for r in range(2)]
        d_gath = [sem(f"d_gath{r}") for r in range(2)]
        p_kv, p_kt, p_ot, p_sim = sem("p_kv"), sem("p_kt"), sem("p_ot"), sem("p_sim")
        p_xt, p_lg, p_rk = sem("p_xt"), sem("p_lg"), sem("p_rk")
        p_g, p_u, p_ht, p_d = sem("p_g"), sem("p_u"), sem("p_ht"), sem("p_d")
        a_kv, a_kc, a_ot, a_tg, a_os = sem("a_kv"), sem("a_kc"), sem("a_ot"), sem("a_tg"), sem("a_os")
        a_th, a_hi, a_exp, a_h, a_hx = sem("a_th"), sem("a_hi"), sem("a_exp"), sem("a_h"), sem("a_hx")
        a_es, a_cs, a_ch = sem("a_es"), sem("a_cs"), sem("a_ch")
        v_chain, v_const, v_gw = sem("v_chain"), sem("v_const"), sem("v_gw")
        v_kc, v_q, v_n, v_nm, v_x1, v_q2, v_ln = (sem(s) for s in "v_kc v_q v_n v_nm v_x1 v_q2 v_ln".split())
        v_h, v_ht, v_xt, v_y = sem("v_h"), sem("v_ht"), sem("v_xt"), sem("v_y")
        v_lg, v_nl, v_m, v_rk, v_mt, v_tab = (sem(s) for s in "v_lg v_nl v_m v_rk v_mt v_tab".split())
        g_chain, g_const = sem("g_chain"), sem("g_const")
        g_r, g_r2, g_lh, g_lx, g_cl, g_ig, g_is = (sem(s) for s in "g_r g_r2 g_lh g_lx g_cl g_ig g_is".split())

        dve_held, pool_held = sem("dve_held"), sem("pool_held")

        block = ctx.enter_context(nc.Block())

        def pair_steps(eng, step):
            step(0, 0, True, False)
            step(1, 1, True, False)
            step(2, 0, True, True)
            with eng.Fori(1, NPAIR // 2 - 1) as k:
                step(2 * k + 1, 1, True, True)
                step(2 * k + 2, 0, True, True)
            step(NPAIR - 1, 1, True, True)
            step(NPAIR, 0, False, True)
            step(NPAIR + 1, 1, False, True)

        def slot_steps(eng, step):
            for s in range(3):
                step(s, s % 2)
            with eng.Fori(1, SLOT_TILES // 2) as k:
                step(2 * k + 1, 1)
                step(2 * k + 2, 0)
            step(SLOT_TILES, 1)

        UNITS_SHARED = NTILE * SHARED_UNITS

        @block.sync
        def _(sp):
            sp.dma_start(wk_sb, wkT).then_inc(d_ctx, 16)
            sp.dma_start(ctx_t, ctxT).then_inc(d_ctx, 16)
            sp.dma_start(bk_sb[:, :], bk).then_inc(d_small, 16)
            sp.dma_start(g_sb[:, :], gates.partition_broadcast(P)).then_inc(d_small, 16)
            sp.dma_start(x_t[:, 0, :, :], xT[0]).then_inc(d_xt[0], 16)
            sp.dma_start(xb[:, 0, :, :], x_pairs[0]).then_inc(d_x[0], 16)
            sp.dma_start(gamma_b, gamma.partition_broadcast(P)).then_inc(d_small, 16)
            sp.dma_start(beta_b, beta.partition_broadcast(P)).then_inc(d_small, 16)
            sp.dma_start(gw[:, :, :], gwT).then_inc(d_gw, 16)
            sp.dma_start(x_t[:, 1, :, :], xT[1]).then_inc(d_xt[1], 16)
            sp.dma_start(xb[:, 1, :, :], x_pairs[1]).then_inc(d_x[1], 16)
            for b in range(2, B):
                sp.dma_start(x_t[:, b, :, :], xT[b]).then_inc(d_xt[b], 16)
            sp.wait_ge(v_const, 1)
            sp.dma_start(meta_d.rearrange("(p c) k -> p (c k)", p=P),
                         fill.rearrange("p c k -> p (c k)")).then_inc(d_fill, 16)
            sp.dma_start(hid_d[T:T + P, :], zero.bitcast(fp16)).then_inc(d_fill, 16)
            sp.dma_start(out[T:T + P, :], zero).then_inc(d_fill, 16)

            def store_out(n, t):
                sp.wait_ge(v_y, 2 * (n - 2) + t + 1)
                sp.dma_start(out_tiles[ds(2 * (n - 2) + t, 1)].rearrange("a p d -> p (a d)"), yb[:, t, :])\
                  .then_inc(d_out[t], 16)

            def step(n, r, att, shared):
                load = att and not (isinstance(n, int) and n in (0, NPAIR - 1))
                if shared:
                    for t in range(2):
                        if t == 1 and not (isinstance(n, int) and n == 2):
                            store_out(n - 1, 1)
                        sp.wait_ge(d_x1w[t], 16 * (n - 1))
                        if not (isinstance(n, int) and n == 2):
                            sp.wait_ge(d_out[t], 16 * (n - 2))
                        sp.dma_start(yb[:, t, :], x1_tiles[ds(2 * (n - 2) + t, 1)].rearrange("a p d -> p (a d)"))\
                          .then_inc(d_x1r[t], 16)
                if load:
                    sp.wait_ge(g_lx, 2 * n)
                    sp.dma_start(xb[:, 1 - r, :, :], x_pairs[ds(n + 1, 1)].rearrange("a p t d -> p (a t) d"))\
                      .then_inc(d_x[1 - r], 16)
                if att:
                    for t in range(2):
                        sp.wait_ge(v_x1, 2 * n + t + 1)
                        sp.dma_start(x1_tiles[ds(2 * n + t, 1)].rearrange("a p d -> p (a d)"), nb[:, t, :])\
                          .then_inc(d_x1w[t], 16)
                if shared:
                    store_out(n, 0)
                if isinstance(n, int) and n == NPAIR:
                    sp.wait_ge(v_tab, 1)
                    sp.wait_ge(d_slots, 64 * NPAIR)
                    load_meta(0, 0)
                    load_meta(1, 1)
                if att:
                    for t in range(2):
                        sp.wait_ge(g_lx, 2 * n + t + 1)
                        sp.dma_start(hid_tiles[ds(2 * n + t, 1)].rearrange("a p d -> p (a d)"),
                                     hl[t].rearrange("p s d -> p (s d)")).then_inc(d_hid[t], 16)
            def load_meta(s, r):
                if not (isinstance(s, int) and s < 2):
                    sp.wait_ge(d_meta[r], 16 * (s // 2) if isinstance(s, int) else 8 * (s - r))
                row = sp.value_load(tr[0:1, ds(s, 1)], min_val=0, max_val=META_ROWS - P)
                sp.dma_start(meta[:, ds(s, 1), :].rearrange("p a k -> p (a k)"), meta_d[ds(row, P), :])\
                  .then_inc(d_meta[r], 16)

            pair_steps(sp, step)
            store_out(NPAIR + 1, 1)
            with sp.Fori(1, TABLE // 2) as k:
                load_meta(2 * k, 0)
                load_meta(2 * k + 1, 1)
            if TABLE % 2:
                load_meta(TABLE - 1, 0)
            sp.wait_ge(d_out[0], 16 * NPAIR)
            sp.wait_ge(d_out[1], 16 * NPAIR)
            sp.wait_ge(d_add, 16 * SLOT_TILES)

        @block.gpsimd
        def _(pool):
            pool.memset(id32, 0.0).then_inc(g_chain, 1)
            pool.memset(id16[:, :], 0.0).then_inc(g_chain, 1)
            pool.memset(ones[:, :], 1.0).then_inc(g_chain, 1)
            pool.wait_ge(g_chain, 3)
            for m in (id32, id16[:, :]):
                pool.affine_select(out=m, in_=m, compare_op=ALU.not_equal, fill=1.0, base=0,
                                   pattern=[[-1, P]], channel_multiplier=1).then_inc(g_const, 1)
            pool.affine_select(out=below[:, :], in_=ones[:, :], compare_op=ALU.is_gt, fill=0.0, base=0,
                               pattern=[[1, P]], channel_multiplier=-1).then_inc(g_const, 1)
            pool.memset(half_m[:, :], -0.5).then_inc(g_const, 1)
            pool.memset(act_hl[:, :, :, F:FP], 0.0).then_inc(g_const, 1)
            pool.memset(before[:, :, :], 0.0).then_inc(g_const, 1)
            pool.iota(i8[:, :, :], [[0, 2], [1, 8]], base=0, channel_multiplier=0).then_inc(g_const, 1)
            pool.iota(sli[:, :, :], [[0, 2], [P, 2]], base=0, channel_multiplier=1).then_inc(g_const, 1)
            pool.iota(te[:, :], [[1, TABLE]], base=0, channel_multiplier=0).then_inc(g_const, 1)
            pool.iota(filla, [[1, META_ROWS // P]], base=0, channel_multiplier=META_ROWS // P).then_inc(g_const, 1)
            pool.memset(fill, 0).then_inc(g_const, 1)
            pool.wait_ge(g_const, 11)

            def conv_low(n, r, u):
                pool.wait_ge(a_ch, 4 * n + u + 1)
                first = isinstance(n, int) and n < 2
                w = ws[:, n, :, :] if first else wr[:, ds(n - 2, 1), :, :].rearrange("p a s n -> p (a s) n")
                c = slice(u * CHUNK, (u + 1) * CHUNK)
                pool.tensor_tensor(w[:, 1, c], stage[:, u % 2, :], w[:, 0, c], ALU.subtract).then_inc(g_cl, 1)

            def low_h(U, p):
                pool.wait_ge(a_hi, U + 1)
                pool.tensor_tensor(act_hl[:, p, 1, 0:F], act_h[:, p, :], act_hl[:, p, 0, 0:F], ALU.subtract)\
                    .then_inc(g_lh, 1)

            def step(n, r, att, shared):
                U = 4 * (n - 2)
                if att:
                    pool.wait_ge(v_q, n + 1)
                    pool.tensor_tensor(r1[:, :], q1[:, :], half_m[:, :], ALU.pow).then_inc(g_r, 1)
                for u in range(2):
                    if shared:
                        low_h(U + u, u % 2)
                    conv_low(n, r, u)
                if shared:
                    low_h(U + 2, 0)
                if att:
                    pool.wait_ge(v_q2, n + 1)
                    pool.tensor_tensor(r2[:, :], q2[:, :], half_m[:, :], ALU.pow).then_inc(g_r2, 1)
                conv_low(n, r, 2)
                if shared:
                    low_h(U + 3, 1)
                if att:
                    for t in range(2):
                        pool.wait_ge(a_hx, 2 * n + t + 1)
                        pool.tensor_tensor(hl[t][:, 1, :], xb[:, r, t, :], hl[t][:, 0, :], ALU.subtract)\
                            .then_inc(g_lx, 1)
                conv_low(n, r, 3)
                if not (isinstance(n, int) and n in (0, NPAIR + 1)):
                    if isinstance(n, int) and n == 1:
                        pool.wait_ge(d_fill, 48)
                    pool.wait_ge(v_mt, n)
                    pool.sem_inc(pool_held, 1)
                    for t in range(2):
                        for c in range(2):
                            pool.indirect_dma_start(
                                out=meta_d, out_offset=bass.IndirectOffsetOnAxis(sli[:, c, t:t + 1], 0),
                                in_=mt[:, t, c, :], in_offset=None).then_inc(d_slots, 16)

            pair_steps(pool, step)

            def gather(s, r):
                pool.wait_ge(d_meta[r], 16 * (s // 2 + 1) if isinstance(s, int) else 8 * (s - r) + 16)
                if not (isinstance(s, int) and s < 2):
                    pool.wait_ge(p_xt, NTILE + s - 1)
                pool.tensor_copy(idxg[:, r:r + 1], meta[:, ds(s, 1), 0:1].rearrange("p a k -> p (a k)"))\
                    .then_inc(g_ig, 1)
                pool.wait_ge(g_ig, s + 1)
                pool.sem_inc(pool_held, 1)
                pool.indirect_dma_start(
                    out=gath[:, r, :, :].rearrange("p s d -> p (s d)"), out_offset=None, in_=hid_d,
                    in_offset=bass.IndirectOffsetOnAxis(idxg[:, r:r + 1], 0)).then_inc(d_gath[r], 16)

            pool.wait_ge(p_u, UNITS_SHARED - 4)
            pool.wait_ge(d_hid[0], 16 * NPAIR)
            pool.wait_ge(d_hid[1], 16 * NPAIR)
            gather(0, 0)
            gather(1, 1)

            def slot_step(s, r):
                if not (isinstance(s, int) and s == SLOT_TILES):
                    gather(s + 2, r)
                    low_h(UNITS_SHARED + s, r)
                if not (isinstance(s, int) and s == 0):
                    pool.tensor_copy(idxs[:, 1 - r:2 - r], meta[:, ds(s - 1, 1), 0:1].rearrange("p a k -> p (a k)"))\
                        .then_inc(g_is, 1)
                    pool.wait_ge(g_is, s)
                    pool.wait_ge(v_y, NTILE + s)
                    if isinstance(s, int) and s == 1:
                        pool.wait_ge(d_out[0], 16 * NPAIR)
                        pool.wait_ge(d_out[1], 16 * NPAIR)
                    else:
                        pool.wait_ge(d_add, 16 * (s - 1))
                    pool.sem_inc(pool_held, 1)
                    pool.indirect_dma_start(
                        out=out, out_offset=bass.IndirectOffsetOnAxis(idxs[:, 1 - r:2 - r], 0),
                        in_=yb[:, 1 - r, :], in_offset=None, compute_op=ALU.add).then_inc(d_add, 16)

            slot_steps(pool, slot_step)

        @block.scalar
        def _(act):
            for c in range(2):
                act.dma_start(stage[:, c, :], wsrc[c]).then_inc(d_st[c], 16)
            act.wait_ge(d_small, 64)
            act.activation(tg[:, :], g_sb[:, :], ACT.Tanh).then_inc(a_tg, 1)

            def prep(b):
                act.wait_ge(p_kv, b + 1)
                act.activation(kvc_t[:, b, :], misc[:, :], ACT.Identity, bias=bk_sb[:, 0:1],
                               accum_out=ksum[:, b:b + 1]).then_inc(a_kv, 1)
                act.wait_ge(p_kt, b + 1)
                act.activation(kvc.rearrange("p c d -> p (c d)"), misc[:, :], ACT.Copy).then_inc(a_kc, 1)
                act.wait_ge(p_ot, b + 1)
                act.activation(out_t[:, b, :], misc[:, :], ACT.Copy).then_inc(a_ot, 1)

            def conv(n, r, u):
                c = 4 * n + u
                act.wait_ge(d_st[u % 2], 16 * (2 * n + u // 2 + 1))
                if isinstance(n, int) and c == 4 * NPAIR:
                    act.wait_ge(p_xt, NTILE)
                    act.wait_ge(g_lx, NTILE)
                    act.wait_ge(d_hid[0], 16 * NPAIR)
                    for t in range(2):
                        act.wait_ge(d_x1w[t], 16 * NPAIR)
                act.activation(stage[:, u % 2, :], stage[:, u % 2, :], ACT.Copy, scale=WSCALE).then_inc(a_cs, 1)
                act.wait_ge(a_cs, c + 1)
                first = isinstance(n, int) and n < 2
                w = ws[:, n, :, :] if first else wr[:, ds(n - 2, 1), :, :].rearrange("p a s n -> p (a s) n")
                act.activation(w[:, 0, u * CHUNK:(u + 1) * CHUNK], stage[:, u % 2, :], ACT.Copy).then_inc(a_ch, 1)
                if isinstance(n, int) and (c == 0 or c == NCHUNK - 1):
                    return
                act.wait_ge(g_cl, c)
                act.dma_start(stage[:, (u + 1) % 2, :], wsrc[ds(c + 1, 1)].rearrange("a p n -> p (a n)"))\
                   .then_inc(d_st[(u + 1) % 2], 16)

            def mlp_act(U, p):
                act.wait_ge(p_g, U + 1)
                act.activation(act_h[:, p, :], g_ps[:, 0:F], ACT.Tanh, scale=0.5 / WSCALE).then_inc(a_th, 1)
                act.wait_ge(v_h, U + 1)
                act.activation(act_hl[:, p, 0, 0:F], act_h[:, p, :], ACT.Copy).then_inc(a_hi, 1)

            prep(0)

            def step(n, r, att, shared):
                U = 4 * (n - 2)
                if att:
                    act.wait_ge(a_ot, n // 2 + 1 if isinstance(n, int) else B)
                    if not (isinstance(n, int) and n == 0):
                        act.wait_ge(p_sim, 2 * n)
                    cols = out_t[:, n // 2, :] if isinstance(n, int) else \
                        out_t[:, ds((n - r) // 2, 1), :].rearrange("p a i -> p (a i)")
                    act.activation(outs.rearrange("p t i -> p (t i)"), cols[:, 2 * P * r:2 * P * (r + 1)],
                                   ACT.Copy).then_inc(a_os, 1)
                if shared:
                    mlp_act(U, 0)
                conv(n, r, 0)
                if shared:
                    mlp_act(U + 1, 1)
                if att:
                    act.wait_ge(v_nm, n + 1)
                    for t in range(2):
                        act.activation(nb[:, t, :], nb[:, t, :], ACT.Exp, bias=ntop[:, t:t + 1],
                                       accum_out=esum[:, t:t + 1]).then_inc(a_exp, 1)
                if isinstance(n, int) and n < 2:
                    prep(n + 1)
                conv(n, r, 1)
                if shared:
                    mlp_act(U + 2, 0)
                if isinstance(n, int) and n == 1:
                    prep(3)
                if not (isinstance(n, int) and n in (0, NPAIR + 1)):
                    act.wait_ge(v_nl, n)
                    for t in range(2):
                        act.activation(es[:, t, :], s8[:, t, :], ACT.Exp, bias=nl[:, t:t + 1], scale=1.0 / WSCALE,
                                       accum_out=ez[:, t:t + 1]).then_inc(a_es, 1)
                conv(n, r, 2)
                if shared:
                    mlp_act(U + 3, 1)
                if att:
                    act.wait_ge(v_ln, n + 1)
                    for t in range(2):
                        act.activation(xb[:, r, t, :], nb[:, t, :], ACT.Identity, bias=nmr[:, t:t + 1],
                                       scale=r2[:, t:t + 1]).then_inc(a_h, 1)
                        act.wait_ge(a_h, 2 * n + t + 1)
                        if not (isinstance(n, int) and n == 0):
                            act.wait_ge(p_xt, 2 * n - 1 + t)
                            act.wait_ge(d_hid[t], 16 * n)
                        act.activation(hl[t][:, 0, :], xb[:, r, t, :], ACT.Copy).then_inc(a_hx, 1)
                conv(n, r, 3)

            pair_steps(act, step)

            def slot_step(s, r):
                if not (isinstance(s, int) and s == SLOT_TILES):
                    mlp_act(UNITS_SHARED + s, r)

            slot_steps(act, slot_step)

        @block.vector
        def _(dve):
            chain = {"base": 0, "n": 0}

            def tick(ins):
                chain["n"] += 1
                ins.then_inc(v_chain, 1)

            def settle():
                dve.wait_ge(v_chain, chain["base"] + chain["n"])

            def held():
                dve.sem_inc(dve_held, 1)

            dve.memset(zero, 0.0).then_inc(v_chain, 1)
            chain["n"] += 1
            dve.wait_ge(g_const, 11)
            tick(dve.tensor_copy(iota8[:, :, :], i8[:, :, :]))
            tick(dve.tensor_copy(tok[:, :], sli[:, 0, :]))
            tick(dve.tensor_copy(iota_s[:, :], te[:, :]))
            tick(dve.tensor_scalar(filla, filla, P - 1, None, ALU.bitwise_and))
            tick(dve.memset(tab[:, 0:2, :], 0.0))
            settle()
            tick(dve.tensor_scalar(first_slot[:, :, :], iota8[:, :, :], float(T), None, ALU.mult))
            dve.tensor_scalar(fill[:, :, 0], filla, float(T), None, ALU.add).then_inc(v_const, 1)

            def center(b):
                dve.wait_ge(a_kv, b + 1)
                tick(dve.tensor_scalar(kmean[:, b:b + 1], ksum[:, b:b + 1], -1.0 / I, None, ALU.mult))
                settle()
                dve.tensor_scalar(kvc_t[:, b, :], kvc_t[:, b, :], kmean[:, b:b + 1], None, ALU.add).then_inc(v_kc, 1)

            center(0)
            dve.wait_ge(a_tg, 1)
            tick(dve.tensor_scalar(tgs[:, :], tg[:, 1:2], 1.0 / WSCALE, None, ALU.mult))
            dve.wait_ge(d_gw, 16)
            tick(dve.tensor_scalar(gwhl[:, 0, :, :], gw[:, :, :], WSCALE, None, ALU.mult))
            settle()
            dve.scalar_tensor_tensor(gwhl[:, 1, :, :].rearrange("p c e -> p (c e)"),
                                     gw[:, :, :].rearrange("p c e -> p (c e)"), WSCALE,
                                     gwhl[:, 0, :, :].rearrange("p c e -> p (c e)"),
                                     ALU.mult, ALU.subtract).then_inc(v_gw, 1)

            def mlp_hidden(U, p):
                dve.wait_ge(a_th, U + 1)
                tick(dve.scalar_tensor_tensor(act_h[:, p, :], act_h[:, p, :], 1.0, g_ps[:, 0:F], ALU.add, ALU.mult))
                settle()
                dve.wait_ge(p_u, U + 1)
                dve.scalar_tensor_tensor(act_h[:, p, :], act_h[:, p, :], 0.5 / WSCALE ** 2, u_ps[:, 0:F],
                                         ALU.mult, ALU.mult).then_inc(v_h, 1)

            def hidden_out(U, p):
                dve.wait_ge(p_ht, U + 1)
                dve.tensor_copy(act_t[:, p, :, :, :], ht_v).then_inc(v_ht, 1)

            def shared_out(n, t):
                dve.wait_ge(p_d, 4 * (n - 2) + 2 * t + 2)
                dve.wait_ge(d_x1r[t], 16 * (n - 1))
                dve.scalar_tensor_tensor(yb[:, t, :], d_ps[:, :], tgs[:, 0:1], yb[:, t, :], ALU.mult, ALU.add)\
                   .then_inc(v_y, 1)

            def tokens_out(m, t, slot):
                dve.wait_ge(p_xt, 2 * m + t + 1)
                dve.tensor_copy(ring[:, slot, t, :, :, :], xt_ps[:, :, :, :]).then_inc(v_xt, 1)

            def attention_stats(n, r):
                dve.wait_ge(d_x[r], 16 * (n // 2 + 1) if isinstance(n, int) else 8 * (n - r) + 16)
                for t in range(2):
                    tick(dve.bn_stats(stx[:, t, :], xb[:, r, t, :]))
                for t in range(2):
                    dve.wait_ge(p_sim, 2 * n + t + 1)
                    tick(dve.bn_stats(sts[:, t, :], sim_ps[:, t, :]))

            def attention_scale():
                settle()
                held()
                for t in range(2):
                    tick(dve.bn_aggr(mvx[:, t, :], stx[:, t, :]))
                    tick(dve.bn_aggr(mvs[:, t, :], sts[:, t, :]))
                settle()
                tick(dve.tensor_scalar(q1a[:, :], mvx[:, :, 1], LN_EPS, SIM_EPS * H, ALU.add, ALU.mult))
                settle()
                dve.tensor_tensor(q1[:, :], q1a[:, :], mvs[:, :, 1], ALU.add).then_inc(v_q, 1)

            def attention_logits(n):
                dve.wait_ge(g_r, n + 1)
                for t in range(2):
                    if not (isinstance(n, int) and n == 0):
                        dve.wait_ge(d_x1w[t], 16 * n)
                    dve.scalar_tensor_tensor(nb[:, t, :], sim_ps[:, t, :], r1[:, t:t + 1], gamma_b,
                                             ALU.mult, ALU.mult).then_inc(v_n, 1)
                for t in range(2):
                    dve.wait_ge(v_n, 2 * n + t + 1)
                    held()
                    tick(dve.tensor_tensor_reduce(out=nb[:, t, :], in0=nb[:, t, :], in1=beta_b, scale=1.0,
                                                  scalar=-3.0e38, op0=ALU.add, op1=ALU.max,
                                                  accum_out=top[:, t:t + 1]))
                settle()
                dve.tensor_scalar(ntop[:, :], top[:, :], -1.0, None, ALU.mult).then_inc(v_nm, 1)

            def attention_add(n, r):
                dve.wait_ge(a_exp, 2 * n + 2)
                tick(dve.reciprocal(rsum[:, :], esum[:, :]))
                settle()
                tick(dve.tensor_scalar(coef[:, :], rsum[:, :], tg[:, 0:1], None, ALU.mult))
                settle()
                for t in range(2):
                    dve.scalar_tensor_tensor(nb[:, t, :], nb[:, t, :], coef[:, t:t + 1], xb[:, r, t, :],
                                             ALU.mult, ALU.add).then_inc(v_x1, 1)
                for t in range(2):
                    dve.wait_ge(v_x1, 2 * n + t + 1)
                    tick(dve.bn_stats(st1[:, t, :], nb[:, t, :]))
                settle()
                held()
                for t in range(2):
                    tick(dve.bn_aggr(mv1[:, t, :], st1[:, t, :]))
                settle()
                dve.tensor_scalar(q2[:, :], mv1[:, :, 1], LN_EPS, None, ALU.add).then_inc(v_q2, 1)

            def attention_norm(n):
                dve.wait_ge(g_r2, n + 1)
                dve.scalar_tensor_tensor(nmr[:, :], mv1[:, :, 0], -1.0, r2[:, :], ALU.mult, ALU.mult).then_inc(v_ln, 1)

            def route_choose(m):
                dve.wait_ge(p_lg, m + 1)
                dve.tensor_copy(lg[:, :, :].rearrange("p t e -> p (t e)"), lg_ps).then_inc(v_lg, 1)
                dve.wait_ge(v_lg, m + 1)
                held()
                for t in range(2):
                    tick(dve.max(s8[:, t, :], lg[:, t, :]))
                settle()
                held()
                for t in range(2):
                    tick(dve.max_index(i8[:, t, :], s8[:, t, :], lg[:, t, :]))
                dve.tensor_scalar(nl[:, :], s8[:, :, 0], -1.0 / WSCALE, None, ALU.mult).then_inc(v_nl, 1)
                settle()
                tick(dve.tensor_copy(idxf[:, :, :], i8[:, :, 0:2]))
                settle()
                for c in range(2):
                    tick(dve.tensor_tensor(mask[:, c, :, :], iota8[:, :, :],
                                           idxf[:, :, c:c + 1].broadcast_to((P, 2, E)), ALU.is_equal))
                settle()
                tick(dve.tensor_tensor(both[:, :, :], mask[:, 0, :, :], mask[:, 1, :, :], ALU.add))
                settle()
                tick(dve.tensor_tensor(before[:, 1, :], before[:, 0, :], both[:, 0, :], ALU.add))
                settle()
                dve.tensor_tensor(before[:, 2, :], before[:, 1, :], both[:, 1, :], ALU.add).then_inc(v_m, 1)

            def route_place(m):
                dve.wait_ge(p_rk, m + 1)
                dve.tensor_tensor(rk[:, :, :].rearrange("p t e -> p (t e)"), rk_ps,
                                  first_slot[:, :, :].rearrange("p t e -> p (t e)"), ALU.add).then_inc(v_rk, 1)
                dve.wait_ge(v_m, m + 1)
                tick(dve.tensor_copy(before[:, 0, :], before[:, 2, :]))
                dve.wait_ge(a_es, 2 * m + 2)
                tick(dve.reciprocal(rz[:, :], ez[:, :]))
                dve.wait_ge(v_rk, m + 1)
                for c in range(2):
                    tick(dve.tensor_tensor(rkm[:, c, :, :], mask[:, c, :, :], rk[:, :, :], ALU.mult))
                settle()
                tick(dve.tensor_reduce(slf[:, :, :].rearrange("p c t -> p (c t)"),
                                       rkm[:, :, :, :].rearrange("p c t e -> p (c t) e"), AX.X, ALU.add))
                tick(dve.tensor_tensor(p12[:, :, :], es[:, :, 0:2], rz[:, :].unsqueeze(2).broadcast_to((P, 2, 2)),
                                       ALU.mult))
                settle()
                if not (isinstance(m, int) and m == 0):
                    dve.wait_ge(d_slots, 64 * m)
                tick(dve.tensor_copy(sli[:, :, :], slf[:, :, :]))
                tick(dve.tensor_reduce(psm[:, :], p12[:, :, :], AX.X, ALU.add))
                settle()
                tick(dve.tensor_scalar(pse[:, :], psm[:, :], 1e-20, None, ALU.add))
                settle()
                tick(dve.reciprocal(prs[:, :], pse[:, :]))
                settle()
                tick(dve.tensor_tensor(mt[:, :, :, 1].bitcast(fp32), p12[:, :, :],
                                       prs[:, :].unsqueeze(2).broadcast_to((P, 2, 2)), ALU.mult))
                for t in range(2):
                    tick(dve.tensor_copy(mt[:, t, :, 0], tok[:, t:t + 1].broadcast_to((P, 2))))
                settle()
                dve.tensor_scalar(tok[:, :], tok[:, :], float(2 * P), None, ALU.add).then_inc(v_mt, 1)

            def slot_tables():
                tick(dve.tensor_scalar(cnt[:, 0, :], tot_ps[0:1, :], float(P - 1), None, ALU.add))
                settle()
                tick(dve.tensor_scalar(cnt[:, 1, :], cnt[:, 0, :], P.bit_length() - 1, None, ALU.arith_shift_right))
                settle()
                tick(dve.tensor_copy(ends[:, 0, :], cnt[:, 1, :]))
                settle()
                for i in range(3):
                    d = 1 << i
                    tick(dve.tensor_copy(ends[:, i + 1, 0:d], ends[:, i, 0:d]))
                    tick(dve.tensor_tensor(ends[:, i + 1, d:E], ends[:, i, d:E], ends[:, i, 0:E - d], ALU.add))
                    settle()
                for e in range(E):
                    end = ends[:, 3, e:e + 1]
                    tick(dve.scalar_tensor_tensor(tab[:, 0, :], iota_s[:, :], end, tab[:, 0, :], ALU.is_ge, ALU.add))
                    tick(dve.tensor_scalar(tab[:, 2, :], iota_s[:, :], end, end, ALU.is_ge, ALU.mult))
                    settle()
                    tick(dve.tensor_tensor(tab[:, 1, :], tab[:, 1, :], tab[:, 2, :], ALU.max))
                    settle()
                tick(dve.tensor_scalar(te[:, :], tab[:, 0, :], float(E - 1), None, ALU.min))
                tick(dve.tensor_tensor(tab[:, 2, :], iota_s[:, :], tab[:, 1, :], ALU.subtract))
                settle()
                tick(dve.tensor_scalar(tab[:, 2, :], tab[:, 2, :], float(P), None, ALU.mult))
                settle()
                dve.scalar_tensor_tensor(tr[:, :], tab[:, 0, :], float(T), tab[:, 2, :], ALU.mult, ALU.add)\
                   .then_inc(v_tab, 1)

            def step(n, r, att, shared):
                U = 4 * (n - 2)
                routed = not (isinstance(n, int) and n in (0, NPAIR + 1))
                piped = shared and not (isinstance(n, int) and n == 2)
                if att:
                    attention_stats(n, r)
                if piped:
                    hidden_out(U - 1, 1)
                if shared:
                    mlp_hidden(U, 0)
                if att:
                    attention_scale()
                if piped:
                    shared_out(n - 1, 1)
                if routed:
                    for t in range(2):
                        tokens_out(n - 1, t, 1 - r)
                if shared:
                    hidden_out(U, 0)
                    mlp_hidden(U + 1, 1)
                if att:
                    attention_logits(n)
                if routed:
                    route_choose(n - 1)
                if isinstance(n, int) and n < 2:
                    center(n + 1)
                if shared:
                    hidden_out(U + 1, 1)
                    mlp_hidden(U + 2, 0)
                    shared_out(n, 0)
                if att:
                    attention_add(n, r)
                if isinstance(n, int) and n == 1:
                    center(3)
                if shared:
                    hidden_out(U + 2, 0)
                    mlp_hidden(U + 3, 1)
                if att:
                    attention_norm(n)
                if routed:
                    route_place(n - 1)
                if isinstance(n, int) and n == NPAIR:
                    slot_tables()

            STEP_TICKS = 43
            step(0, 0, True, False)
            step(1, 1, True, False)
            step(2, 0, True, True)
            before_loop = chain["n"]
            with dve.Fori(1, NPAIR // 2 - 1) as k:
                chain["base"], chain["n"] = before_loop + (k - 1) * (2 * STEP_TICKS), 0
                step(2 * k + 1, 1, True, True)
                step(2 * k + 2, 0, True, True)
                assert chain["n"] == 2 * STEP_TICKS, chain["n"]
            chain["base"], chain["n"] = 0, before_loop + (NPAIR // 2 - 2) * 2 * STEP_TICKS
            step(NPAIR - 1, 1, True, True)
            step(NPAIR, 0, False, True)
            step(NPAIR + 1, 1, False, True)

            def slot_tokens_out(s, r):
                dve.wait_ge(p_xt, NTILE + s + 1)
                dve.tensor_copy(xg_t[:, r, :, :, :], xt_ps[:, :, :, :]).then_inc(v_xt, 1)

            def slot_step(s, r):
                U = UNITS_SHARED + s
                hidden_out(U - 1, 1 - r)
                if not (isinstance(s, int) and s == SLOT_TILES):
                    slot_tokens_out(s + 1, 1 - r)
                    mlp_hidden(U, r)
                if isinstance(s, int) and s == 0:
                    shared_out(NPAIR + 1, 1)
                    return
                dve.wait_ge(p_d, U)
                if isinstance(s, int) and s < 3:
                    dve.wait_ge(d_out[s - 1], 16 * NPAIR)
                else:
                    dve.wait_ge(d_add, 16 * (s - 2))
                w = meta[:, ds(s - 1, 1), 1:2].rearrange("p a k -> p (a k)").bitcast(fp32)
                dve.tensor_scalar(yb[:, 1 - r, :], d_ps[:, :], w, tgs[:, 0:1], ALU.mult, ALU.mult).then_inc(v_y, 1)

            slot_tokens_out(0, 0)
            head = chain["n"]
            for s in range(3):
                slot_step(s, s % 2)
            assert chain["n"] == head + 3
            with dve.Fori(1, SLOT_TILES // 2) as k:
                chain["base"], chain["n"] = head + 3 + (k - 1) * 2, 0
                slot_step(2 * k + 1, 1)
                slot_step(2 * k + 2, 0)
            chain["base"], chain["n"] = 0, head + 3 + (SLOT_TILES // 2 - 1) * 2
            slot_step(SLOT_TILES, 1)

        @block.tensor
        def _(pe):
            PRODUCTS = ((0, 0), (0, 1), (1, 0))

            def prep(b):
                pe.matmul(misc[:, :], wk_sb, ctx_t[:, b, :], start=True, stop=True).then_inc(p_kv, 1)
                pe.wait_ge(v_kc, b + 1)
                for c in range(HC):
                    mm = pe.transpose(misc[:, c * P:(c + 1) * P], kvc_t[:, b, c * P:(c + 1) * P], id32)
                mm.then_inc(p_kt, 1)
                pe.wait_ge(a_kc, b + 1)
                pe.wait_ge(d_xt[b], 16)
                for c in range(HC):
                    mm = pe.matmul(misc[:, :], kvc[:, c, :], x_t[:, b, c, :], start=(c == 0), stop=(c == HC - 1))
                mm.then_inc(p_ot, 1)

            def sims(n, r):
                pe.wait_ge(a_os, n + 1)
                kv = kvc_t[:, n // 2, :] if isinstance(n, int) else \
                    kvc_t[:, ds((n - r) // 2, 1), :].rearrange("p a i -> p (a i)")
                for t in range(2):
                    if not (isinstance(n, int) and n == 0):
                        pe.wait_ge(v_n, 2 * n - 1 + t)
                    pe.matmul(sim_ps[:, t, :], outs[:, t, :], kv, start=True, stop=True).then_inc(p_sim, 1)

            def transpose_tokens(src):
                for h in range(2):
                    for c in range(HC):
                        mm = pe.transpose(xt_ps[:, h, c, :], src[:, h, c * P:(c + 1) * P], id16[:, :])
                mm.then_inc(p_xt, 1)

            def pair_tokens(m, t):
                pe.wait_ge(g_lx, 2 * m + t + 1)
                if not (isinstance(m, int) and m == 0 and t == 0):
                    pe.wait_ge(v_xt, 2 * m + t)
                transpose_tokens(hl[t])

            def router_logits(m, slot):
                pe.wait_ge(v_xt, 2 * m + 2)
                if isinstance(m, int) and m == 0:
                    pe.wait_ge(v_gw, 1)
                    pe.wait_ge(a_ot, 2)
                else:
                    pe.wait_ge(v_rk, m)
                for t in range(2):
                    for c in range(HC):
                        for i, (a, b) in enumerate(PRODUCTS):
                            mm = pe.matmul(lg_ps[:, t * E:(t + 1) * E], ring[:, slot, t, a, c, :], gwhl[:, b, c, :],
                                           start=(c == 0 and i == 0), stop=(c == HC - 1 and i == 2))
                mm.then_inc(p_lg, 1)

            def router_ranks(m):
                pe.wait_ge(v_m, m + 1)
                pe.matmul(rk_ps, below[:, :], both[:, :, :].rearrange("p t e -> p (t e)"), start=True, stop=False)
                mm = pe.matmul(rk_ps, ones[:, :], before[:, 0:2, :].rearrange("p t e -> p (t e)"), start=False, stop=True)
                if isinstance(m, int) and m == NPAIR - 1:
                    mm = pe.matmul(tot_ps, ones[:, :], before[:, 2, :], start=True, stop=True)
                mm.then_inc(p_rk, 1)

            def up_or_gate(ps, at, xs, w):
                for c in range(HC):
                    for i, (a, b) in enumerate(PRODUCTS):
                        mm = pe.matmul(ps[:, 0:F], xs[:, a, c, :], w[:, b, at + c * F:at + (c + 1) * F],
                                       start=(c == 0 and i == 0), stop=(c == HC - 1 and i == 2))
                return mm

            def gate(xs, w):
                up_or_gate(g_ps, GATE, xs, w).then_inc(p_g, 1)

            def up(xs, w):
                up_or_gate(u_ps, UP, xs, w).then_inc(p_u, 1)

            def transpose_hidden(U, p):
                pe.wait_ge(g_lh, U + 1)
                for h in range(2):
                    for c in range(FC):
                        mm = pe.transpose(ht_v[:, h, c, :], act_hl[:, p, h, c * P:(c + 1) * P], id16[:, :])
                mm.then_inc(p_ht, 1)

            def down(U, p, w, first, last):
                pe.wait_ge(v_ht, U + 1)
                for c in range(FC):
                    for i, (a, b) in enumerate(PRODUCTS):
                        mm = pe.matmul(d_ps[:, :], act_t[:, p, a, c, :], w[:, b, DOWN + c * H:DOWN + (c + 1) * H],
                                       start=(first and c == 0 and i == 0), stop=(last and c == FC - 1 and i == 2))
                mm.then_inc(p_d, 1)

            pe.wait_ge(g_const, 11)
            pe.wait_ge(d_ctx, 32)
            prep(0)

            def step(n, r, att, shared):
                U = 4 * (n - 2)
                routed = not (isinstance(n, int) and n in (0, NPAIR + 1))

                def xs(t):
                    return ring[:, r, t, :, :, :]

                def unit(u):
                    piped = not (isinstance(n, int) and n == 2 and u == 0)
                    if piped:
                        pe.wait_ge(v_h, U + u)
                    gate(xs(u // 2), ws[:, u % 2, :, :])
                    if piped:
                        transpose_hidden(U + u - 1, (u - 1) % 2)
                    up(xs(u // 2), ws[:, u % 2, :, :])
                    if piped:
                        if u == 3:
                            pe.wait_ge(v_y, 2 * (n - 2) + 1)
                        down(U + u - 1, (u - 1) % 2, ws[:, (u - 1) % 2, :, :], u % 2 == 1, u % 2 == 0)

                if isinstance(n, int) and n == 0:
                    sims(0, 0)
                if shared:
                    pe.wait_ge(v_xt, 2 * (n - 1))
                    pe.wait_ge(g_cl, SHARED_UNITS * QUARTERS)
                    unit(0)
                if routed:
                    pair_tokens(n - 1, 0)
                    pair_tokens(n - 1, 1)
                if shared:
                    unit(1)
                if routed:
                    router_logits(n - 1, 1 - r)
                if isinstance(n, int) and n == 0:
                    pe.wait_ge(a_ot, 1)
                    prep(1)
                if isinstance(n, int) and n == 1:
                    pe.wait_ge(v_lg, 1)
                    prep(2)
                    pe.wait_ge(a_ot, 3)
                    prep(3)
                    pe.wait_ge(a_ot, 4)
                if shared:
                    unit(2)
                if routed:
                    router_ranks(n - 1)
                if shared:
                    unit(3)
                if att and not (isinstance(n, int) and n == NPAIR - 1):
                    sims(n + 1, 1 - r)

            pair_steps(pe, step)

            def expert(s):
                e = pe.value_load(te[0:1, ds(s, 1)], min_val=0, max_val=E - 1)
                return wr[:, ds(e, 1), :, :].rearrange("p a s n -> p (a s) n")

            def slot_tokens(s, r):
                pe.wait_ge(d_gath[r], 16 * (s // 2 + 1) if isinstance(s, int) else 8 * (s - r) + 16)
                pe.wait_ge(v_xt, NTILE + s)
                transpose_tokens(gath[:, r, :, :])

            pe.wait_ge(v_tab, 1)
            pe.wait_ge(g_cl, NCHUNK)
            slot_tokens(0, 0)

            def slot_step(s, r):
                U = UNITS_SHARED + s
                last, first = isinstance(s, int) and s == SLOT_TILES, isinstance(s, int) and s == 0
                if not last:
                    w = expert(s)
                    pe.wait_ge(v_xt, NTILE + s + 1)
                    pe.wait_ge(v_h, U)
                    gate(xg_t[:, r, :, :, :], w)
                transpose_hidden(U - 1, 1 - r)
                if not last:
                    slot_tokens(s + 1, 1 - r)
                    up(xg_t[:, r, :, :, :], w)
                if first:
                    down(U - 1, 1, ws[:, 1, :, :], False, True)
                else:
                    w = expert(s - 1)
                    pe.wait_ge(v_y, NTILE + s - 1)
                    down(U - 1, 1 - r, w, True, True)

            slot_steps(pe, slot_step)


_OUTS = [((T + P, H), "float32")]


def kernel(**inputs):
    import numpy as np
    import concourse.bacc as bacc
    from concourse.bass_utils import run_bass_kernel_spmd

    a = {k: np.asarray(v) for k, v in inputs.items()}

    def unit(gate, up, down):
        parts = [m.T.reshape(HC, P, F).transpose(1, 0, 2).reshape(P, HC * F) for m in (gate, up)]
        d = np.zeros((FP, H), down.dtype)
        d[0:F] = down.T
        parts.append(d.reshape(FC, P, H).transpose(1, 0, 2).reshape(P, FC * H))
        return np.concatenate(parts, axis=1)

    sg, su, sd = a["L0_ffn_sw_gate"], a["L0_ffn_sw_up"], a["L0_ffn_sw_down"]
    units = [unit(sg[i * F:(i + 1) * F], su[i * F:(i + 1) * F], sd[:, i * F:(i + 1) * F]) for i in range(SHARED_UNITS)]
    units += [unit(a["L0_ffn_w_gate"][e], a["L0_ffn_w_up"][e], a["L0_ffn_w_down"][e]) for e in range(E)]
    wsrc = np.stack(units).reshape(SHARED_UNITS + E, P, QUARTERS, CHUNK).transpose(0, 2, 1, 3).reshape(NCHUNK, P, CHUNK)
    arrays = {
        "x": a["x"].reshape(T, H),
        "xT": a["x"].transpose(0, 2, 1).reshape(B, HC, P, I).transpose(0, 2, 1, 3),
        "ctxT": a["ctx_512"].transpose(2, 0, 1),
        "wkT": a["L0_xattn_W_k"].T,
        "bk": a["L0_xattn_b_k"].reshape(DC, 1),
        "gates": np.concatenate([a["g_xattn"], a["g_ffn"]]),
        "gamma": a["L0_xattn_ln_gamma"],
        "beta": a["L0_xattn_ln_beta"],
        "gwT": a["L0_ffn_gate_weight"].T.reshape(HC, P, E).transpose(1, 0, 2),
        "wsrc": wsrc,
    }
    nc = bacc.Bacc("TRN2", target_bir_lowering=False, num_devices=1)
    args = []
    for name in arrays:
        arrays[name] = np.ascontiguousarray(arrays[name])
        args.append(nc.dram_tensor(name, arrays[name].shape, mybir.dt.from_np(arrays[name].dtype),
                                   kind="ExternalInput").ap())
    shape, dtype = _OUTS[0]
    args.append(nc.dram_tensor("out", shape, mybir.dt.from_np(np.dtype(dtype)), kind="ExternalOutput").ap())
    flamingo_block(nc, *args)
    r = run_bass_kernel_spmd(nc, [arrays], core_ids=[0])
    return r.results[0]["out"][0:T].reshape(B, I, H)
```

```python
import concourse.bass as bass
from concourse import mybir
from contextlib import ExitStack

B, I, H = 4, 512, 512
DC = 128
E, F, TOPK = 8, 352, 2
P = 128
T = B * I
NTILE = T // P
NPAIR = NTILE // 2
HC = H // P
FC = -(-F // P)
FP = FC * P
GATE, UP, DOWN = 0, HC * F, 2 * HC * F
UNIT = DOWN + FC * H
QUARTERS = 4
CHUNK = UNIT // QUARTERS
SHARED_UNITS = 2
SHARED_CHUNKS, EXPERT_CHUNKS = SHARED_UNITS * QUARTERS, E * QUARTERS
NCHUNK = SHARED_CHUNKS + EXPERT_CHUNKS
SLOT_TILES = (T * TOPK + E * (P - 1)) // P
AHEAD = 2
TABLE = SLOT_TILES + AHEAD
META_ROWS = E * T + 10 * P
LN_EPS, SIM_EPS = 1e-5, 1e-6
WSCALE = 256.0


def flamingo_block(nc, x, xT, ctxT, wkT, bk, gates, gamma, beta, gwT, wsrc, out):
    fp32, fp16 = mybir.dt.float32, mybir.dt.float16
    i32, u32 = mybir.dt.int32, mybir.dt.uint32
    ALU, ACT, AX = mybir.AluOpType, mybir.ActivationFunctionType, mybir.AxisListType
    ds = bass.ds

    x1_d = nc.dram_tensor("x1_d", (T, H), fp32, kind="Internal").ap()
    hid_d = nc.dram_tensor("hid_d", (T + P, 2 * H), fp16, kind="Internal").ap()
    meta_d = nc.dram_tensor("meta_d", (META_ROWS, 2), i32, kind="Internal").ap()

    def by_tile(ap):
        return ap[0:T, :].rearrange("(n p) d -> n p d", p=P)

    x_pairs = x.rearrange("(n t p) d -> n p t d", t=2, p=P)
    x1_tiles, hid_tiles, out_tiles = by_tile(x1_d), by_tile(hid_d), by_tile(out)

    ctx = ExitStack()
    with ctx:
        def sb(name, shape, dt):
            return ctx.enter_context(nc.sbuf_tensor(name, shape, dt))

        def pb(name, shape, dt):
            return ctx.enter_context(nc.psum_tensor(name, shape, dt))

        def sem(name):
            return ctx.enter_context(nc.semaphore(name))

        ws = sb("ws", [P, SHARED_UNITS, 2, UNIT], fp16)
        wr = sb("wr", [P, E, 2, UNIT], fp16)

        def overlay(expert, offset, words, dt=fp32):
            flat = wr[:, :, :, :].rearrange("p e s n -> p (e s n)")
            at = expert * 2 * UNIT + 2 * offset
            v = flat[:, at:at + 2 * words]
            return v if dt == fp16 else v.bitcast(dt)

        ctx_t = overlay(3, 0, B * I).rearrange("p (b i) -> p b i", b=B)
        x_t = overlay(4, 0, B * HC * I).rearrange("p (b c i) -> p b c i", b=B, c=HC)
        kvc = [overlay(4, B * HC * I, HC * DC).rearrange("p (c d) -> p c d", c=HC),
               overlay(3, B * I + 1312, HC * DC).rearrange("p (c d) -> p c d", c=HC)]
        kvc_t = overlay(6, 0, B * I).rearrange("p (b i) -> p b i", b=B)
        out_t = overlay(6, B * I, B * I).rearrange("p (b i) -> p b i", b=B)
        xb = overlay(6, 2 * B * I, 4 * H).rearrange("p (r t d) -> p r t d", r=2, t=2)
        nb = overlay(6, 2 * B * I + 4 * H, 2 * H).rearrange("p (t d) -> p t d", t=2)
        gamma_b = overlay(6, 2 * B * I + 6 * H, H)
        beta_b = overlay(6, 2 * B * I + 7 * H, H)
        hl0 = overlay(6, 2 * B * I + 8 * H, H, fp16).rearrange("p (s d) -> p s d", s=2)

        stage_s = overlay(1, 0, SHARED_CHUNKS * CHUNK).rearrange("p (c n) -> p c n", c=SHARED_CHUNKS)
        stage = sb("stage", [P, 2, CHUNK], fp32)
        ring = sb("ring", [P, 2, 2, 2, HC, P], fp16)
        xg_t = sb("xg_t", [P, 2, 2, HC, P], fp16)
        hl1 = xg_t[:, 1, :, :, :].rearrange("p s c n -> p s (c n)")
        outs = xg_t[:, 0, :, :, :].rearrange("p s c n -> p (s c n)").bitcast(fp32)[:, 0:2 * P]\
            .rearrange("p (t i) -> p t i", t=2)
        act_h = sb("act_h", [P, 2, F], fp32)
        act_hl = sb("act_hl", [P, 2, 2, FP], fp16)
        act_t = sb("act_t", [P, 2, 2, FC, P], fp16)
        yb = sb("yb", [P, 2, H], fp32)
        gath = ring[:, 0, :, :, :, :].rearrange("p t s c n -> p t s (c n)")
        hl = [hl0, hl1]

        id32 = overlay(3, B * I + 1024, P)
        id16 = sb("id16", [P, P], fp16)
        below = sb("below", [P, P], fp16)
        ones = sb("ones", [P, P], fp16)
        wk_sb = overlay(3, B * I + 1152, DC)
        bk_sb = sb("bk_sb", [P, 1], fp32)
        ksum = sb("ksum", [P, B], fp32)
        kmean = sb("kmean", [P, B], fp32)
        g_sb = sb("g_sb", [P, 2], fp32)
        tg = sb("tg", [P, 2], fp32)
        tgs = sb("tgs", [P, 1], fp32)
        table = sb("table", [P, 2], fp32)
        gw = overlay(3, B * I + 1280, HC * E).rearrange("p (c e) -> p c e", c=HC)
        gwhl = sb("gwhl", [P, 2, HC, E], fp16)
        half_m = sb("half_m", [P, 2], fp32)
        stx = sb("stx", [P, 2, 6], fp32)
        sts = sb("sts", [P, 2, 6], fp32)
        st1 = sb("st1", [P, 2, 6], fp32)
        mvx = sb("mvx", [P, 2, 2], fp32)
        mvs = sb("mvs", [P, 2, 2], fp32)
        mv1 = sb("mv1", [P, 2, 2], fp32)
        q1a = sb("q1a", [P, 2], fp32)
        q1 = sb("q1", [P, 2], fp32)
        r1 = sb("r1", [P, 2], fp32)
        q2 = sb("q2", [P, 2], fp32)
        r2 = sb("r2", [P, 2], fp32)
        nmr = sb("nmr", [P, 2], fp32)
        top = sb("top", [P, 2], fp32)
        ntop = sb("ntop", [P, 2], fp32)
        esum = sb("esum", [P, 2], fp32)
        rsum = sb("rsum", [P, 2], fp32)
        coef = sb("coef", [P, 2], fp32)
        lg = sb("lg", [P, 2, E], fp32)
        s8 = sb("s8", [P, 2, 8], fp32)
        i8 = sb("i8", [P, 2, 8], u32)
        idxf = sb("idxf", [P, 2, 2], fp32)
        iota8 = sb("iota8", [P, 2, E], fp32)
        mask = sb("mask", [P, 2, 2, E], fp32)
        both = sb("both", [P, 2, E], fp16)
        before = sb("before", [P, 3, E], fp16)
        nl = sb("nl", [P, 2], fp32)
        es = sb("es", [P, 2, 8], fp32)
        ez = sb("ez", [P, 2], fp32)
        rz = sb("rz", [P, 2], fp32)
        p12 = sb("p12", [P, 2, 2], fp32)
        psm = sb("psm", [P, 2], fp32)
        pse = sb("pse", [P, 2], fp32)
        prs = sb("prs", [P, 2], fp32)
        first_slot = sb("first_slot", [P, 2, E], fp32)
        rk = sb("rk", [P, 2, E], fp32)
        rkm = sb("rkm", [P, 2, 2, E], fp32)
        slf = sb("slf", [P, 2, 2], fp32)
        sli = sb("sli", [P, 2, 2], i32)
        tok = sb("tok", [P, 2], fp32)
        mt = sb("mt", [P, 2, 2, 2], i32)
        fill = overlay(3, B * I, 2 * (META_ROWS // P), i32).rearrange("p (c k) -> p c k", k=2)
        filla = overlay(3, B * I + 324, META_ROWS // P, i32)
        zero = overlay(3, B * I + 512, H, fp32)
        meta = sb("meta", [P, TABLE, 2], i32)
        idxg = sb("idxg", [P, 2], i32)
        idxs = sb("idxs", [P, 2], i32)
        cnt = sb("cnt", [1, 2, E], i32)
        tiles = sb("tiles", [1, E], fp32)
        ends = sb("ends", [1, 4, E], fp32)
        iota_s = sb("iota_s", [1, TABLE], fp32)
        tab = sb("tab", [1, 3, TABLE], fp32)
        te = sb("te", [1, TABLE], i32)
        tr = sb("tr", [1, TABLE], i32)

        misc = pb("misc", [P, 512], fp32)
        sim_ps = pb("sim_ps", [P, 2, 512], fp32)
        g_ps = pb("g_ps", [P, 512], fp32)
        u_ps = pb("u_ps", [P, 512], fp32)
        d_ps = pb("d_ps", [P, 512], fp32)
        xt_ps = pb("xt_ps", [P, 2, HC, P], fp16)
        ht_ps = pb("ht_ps", [P, 1024], fp16)
        ht_v = ht_ps[:, 0:2 * FP].rearrange("p (s c n) -> p s c n", s=2, c=FC)
        lg_ps = misc[:, 0:2 * E]
        rk_ps = misc[:, 32:32 + 2 * E]
        tot_ps = misc[:, 64:64 + E]
        prep_ps = [misc, g_ps, u_ps, d_ps]
        past = sim_ps[0:1, 0, 0:TABLE * E].rearrange("p (s e) -> p s e", e=E)
        past_end = sim_ps[0:1, 1, 0:TABLE * E].rearrange("p (s e) -> p s e", e=E)

        d_wk, d_bk, d_gates, d_gb, d_gw = sem("d_wk"), sem("d_bk"), sem("d_gates"), sem("d_gb"), sem("d_gw")
        d_ctx = [sem(f"d_ctx{b}") for b in range(B)]
        d_ws = [sem(f"d_ws{i}") for i in range(SHARED_CHUNKS // 2)]
        d_xt = [sem(f"d_xt{b}") for b in range(B)]
        d_x = [sem(f"d_x{r}") for r in range(2)]
        d_st = [sem(f"d_st{r}") for r in range(2)]
        d_x1w = [sem(f"d_x1w{t}") for t in range(2)]
        d_x1r = [sem(f"d_x1r{t}") for t in range(2)]
        d_hid = [sem(f"d_hid{t}") for t in range(2)]
        d_out = [sem(f"d_out{t}") for t in range(2)]
        d_fill, d_slots, d_add = sem("d_fill"), sem("d_slots"), sem("d_add")
        d_meta = [sem(f"d_meta{r}") for r in range(2)]
        d_gath = [sem(f"d_gath{r}") for r in range(2)]
        p_kv, p_kt, p_ot, p_sim = sem("p_kv"), sem("p_kt"), sem("p_ot"), sem("p_sim")
        p_xt, p_lg, p_rk = sem("p_xt"), sem("p_lg"), sem("p_rk")
        p_g, p_u, p_ht, p_d = sem("p_g"), sem("p_u"), sem("p_ht"), sem("p_d")
        a_kv, a_kc, a_ot, a_tg, a_os = sem("a_kv"), sem("a_kc"), sem("a_ot"), sem("a_tg"), sem("a_os")
        a_th, a_hi, a_exp, a_h, a_hx = sem("a_th"), sem("a_hi"), sem("a_exp"), sem("a_h"), sem("a_hx")
        a_es, a_cs, a_ch, a_wh, a_table = sem("a_es"), sem("a_cs"), sem("a_ch"), sem("a_wh"), sem("a_table")
        v_wl, v_cl = sem("v_wl"), sem("v_cl")
        v_chain, v_const, v_gw = sem("v_chain"), sem("v_const"), sem("v_gw")
        v_kc, v_q, v_n, v_nm, v_x1, v_q2, v_ln = (sem(s) for s in "v_kc v_q v_n v_nm v_x1 v_q2 v_ln".split())
        v_h, v_ht, v_xt, v_y = sem("v_h"), sem("v_ht"), sem("v_xt"), sem("v_y")
        v_lg, v_nl, v_m, v_rk, v_mt, v_tab = (sem(s) for s in "v_lg v_nl v_m v_rk v_mt v_tab".split())
        g_chain, g_const = sem("g_chain"), sem("g_const")
        g_r, g_r2, g_lh, g_lx, g_cl, g_ig, g_is = (sem(s) for s in "g_r g_r2 g_lh g_lx g_cl g_ig g_is".split())

        dve_held, pool_held, sp_held = sem("dve_held"), sem("pool_held"), sem("sp_held")

        block = ctx.enter_context(nc.Block())

        def pair_steps(eng, step):
            step(1, 1)
            step(2, 0)
            with eng.Fori(1, NPAIR // 2 - 1) as k:
                step(2 * k + 1, 1)
                step(2 * k + 2, 0)
            step(NPAIR - 1, 1)

        def first_unit(n):
            return 4 * (n - 1) - 1

        def places(n):
            return range(1, 4) if isinstance(n, int) and n == 1 else range(4)

        def slot_steps(eng, step):
            for s in range(3):
                step(s, s % 2)
            with eng.Fori(1, SLOT_TILES // 2) as k:
                step(2 * k + 1, 1)
                step(2 * k + 2, 0)
            step(SLOT_TILES, 1)

        UNITS_SHARED = NTILE * SHARED_UNITS

        @block.sync
        def _(sp):
            def load(to, what, signal):
                sp.dma_start(to, what).then_inc(signal, 16)

            load(wk_sb, wkT, d_wk)
            load(ctx_t[:, 0, :], ctxT[:, 0, :], d_ctx[0])
            load(bk_sb[:, :], bk, d_bk)
            load(x_t[:, 0, :, :], xT[0], d_xt[0])
            load(xb[:, 0, :, :], x_pairs[0], d_x[0])
            load(ctx_t[:, 1, :], ctxT[:, 1, :], d_ctx[1])
            load(g_sb[:, :], gates.partition_broadcast(P), d_gates)
            load(gamma_b, gamma.partition_broadcast(P), d_gb)
            load(beta_b, beta.partition_broadcast(P), d_gb)
            for i in range(SHARED_CHUNKS // 2):
                if i > 1:
                    load(ctx_t[:, i, :], ctxT[:, i, :], d_ctx[i])
                    load(x_t[:, i - 1, :, :], xT[i - 1], d_xt[i - 1])
                load(stage_s[:, 2 * i:2 * i + 2, :], wsrc[2 * i:2 * i + 2].rearrange("c p n -> p c n"), d_ws[i])
            load(gw[:, :, :], gwT, d_gw)
            load(xb[:, 1, :, :], x_pairs[1], d_x[1])
            load(x_t[:, 3, :, :], xT[3], d_xt[3])
            sp.wait_ge(v_const, 1)
            sp.dma_start(meta_d.rearrange("(p c) k -> p (c k)", p=P),
                         fill.rearrange("p c k -> p (c k)")).then_inc(d_fill, 16)
            sp.dma_start(hid_d[T:T + P, :], zero.bitcast(fp16)).then_inc(d_fill, 16)
            sp.dma_start(out[T:T + P, :], zero).then_inc(d_fill, 16)

            def store_x1(n):
                for t in range(2):
                    sp.wait_ge(v_x1, 2 * n + t + 1)
                    sp.dma_start(x1_tiles[ds(2 * n + t, 1)].rearrange("a p d -> p (a d)"), nb[:, t, :])\
                      .then_inc(d_x1w[t], 16)

            def store_tokens(n):
                for t in range(2):
                    sp.wait_ge(g_lx, 2 * n + t + 1)
                    sp.dma_start(hid_tiles[ds(2 * n + t, 1)].rearrange("a p d -> p (a d)"),
                                 hl[t].rearrange("p s d -> p (s d)")).then_inc(d_hid[t], 16)

            def load_x1(m, t):
                if not (isinstance(m, int) and m == 0):
                    sp.wait_ge(d_out[t], 16 * m)
                    sp.sem_inc(sp_held, 1)
                sp.wait_ge(d_x1w[t], 16 * (m + 1))
                sp.dma_start(yb[:, t, :], x1_tiles[ds(2 * m + t, 1)].rearrange("a p d -> p (a d)"))\
                  .then_inc(d_x1r[t], 16)

            def store_out(m, t):
                sp.wait_ge(v_y, 2 * m + t + 1)
                sp.dma_start(out_tiles[ds(2 * m + t, 1)].rearrange("a p d -> p (a d)"), yb[:, t, :])\
                  .then_inc(d_out[t], 16)

            def step(n, r):
                if not (isinstance(n, int) and n == NPAIR - 1):
                    sp.wait_ge(g_lx, 2 * n)
                    sp.dma_start(xb[:, 1 - r, :, :], x_pairs[ds(n + 1, 1)].rearrange("a p t d -> p (a t) d"))\
                      .then_inc(d_x[1 - r], 16)
                load_x1(n - 1, 0)
                if not (isinstance(n, int) and n == 1):
                    store_out(n - 2, 1)
                load_x1(n - 1, 1)
                store_x1(n)
                store_tokens(n)
                store_out(n - 1, 0)

            def load_meta(s, r):
                if not (isinstance(s, int) and s < 2):
                    sp.wait_ge(d_meta[r], 16 * (s // 2) if isinstance(s, int) else 8 * (s - r))
                row = sp.value_load(tr[0:1, ds(s, 1)], min_val=0, max_val=META_ROWS - P)
                sp.dma_start(meta[:, ds(s, 1), :].rearrange("p a k -> p (a k)"), meta_d[ds(row, P), :])\
                  .then_inc(d_meta[r], 16)

            store_x1(0)
            store_tokens(0)
            pair_steps(sp, step)
            load_x1(NPAIR - 1, 0)
            store_out(NPAIR - 2, 1)
            load_x1(NPAIR - 1, 1)
            sp.wait_ge(v_tab, 1)
            sp.wait_ge(d_slots, 64 * NPAIR)
            load_meta(0, 0)
            load_meta(1, 1)
            store_out(NPAIR - 1, 0)
            with sp.Fori(1, TABLE // 2) as k:
                load_meta(2 * k, 0)
                load_meta(2 * k + 1, 1)
            if TABLE % 2:
                load_meta(TABLE - 1, 0)
            sp.wait_ge(d_out[0], 16 * NPAIR)
            sp.wait_ge(d_out[1], 16 * NPAIR)
            sp.wait_ge(d_add, 16 * SLOT_TILES)

        @block.gpsimd
        def _(pool):
            pool.memset(id32, 0.0).then_inc(g_chain, 1)
            pool.memset(id16[:, :], 0.0).then_inc(g_chain, 1)
            pool.memset(ones[:, :], 1.0).then_inc(g_chain, 1)
            pool.wait_ge(g_chain, 3)
            for m in (id32, id16[:, :]):
                pool.affine_select(out=m, in_=m, compare_op=ALU.not_equal, fill=1.0, base=0,
                                   pattern=[[-1, P]], channel_multiplier=1).then_inc(g_const, 1)
            pool.affine_select(out=below[:, :], in_=ones[:, :], compare_op=ALU.is_gt, fill=0.0, base=0,
                               pattern=[[1, P]], channel_multiplier=-1).then_inc(g_const, 1)
            pool.memset(half_m[:, :], -0.5).then_inc(g_const, 1)
            pool.memset(act_hl[:, :, :, F:FP], 0.0).then_inc(g_const, 1)
            pool.memset(before[:, :, :], 0.0).then_inc(g_const, 1)
            pool.iota(i8[:, :, :], [[0, 2], [1, 8]], base=0, channel_multiplier=0).then_inc(g_const, 1)
            pool.iota(sli[:, :, :], [[0, 2], [P, 2]], base=0, channel_multiplier=1).then_inc(g_const, 1)
            pool.iota(te[:, :], [[1, TABLE]], base=0, channel_multiplier=0).then_inc(g_const, 1)
            pool.iota(filla, [[1, META_ROWS // P]], base=0, channel_multiplier=META_ROWS // P).then_inc(g_const, 1)
            pool.memset(fill, 0).then_inc(g_const, 1)
            pool.wait_ge(g_const, 11)

            def conv_low(n, u):
                pool.wait_ge(a_ch, 4 * (n - 1) + u + 1)
                w = wr[:, ds(n - 1, 1), :, :].rearrange("p a s n -> p (a s) n")
                c = slice(u * CHUNK, (u + 1) * CHUNK)
                pool.tensor_tensor(w[:, 1, c], stage[:, u % 2, :], w[:, 0, c], ALU.subtract).then_inc(g_cl, 1)

            def low_h(U, p):
                pool.wait_ge(a_hi, U + 1)
                pool.tensor_tensor(act_hl[:, p, 1, 0:F], act_h[:, p, :], act_hl[:, p, 0, 0:F], ALU.subtract)\
                    .then_inc(g_lh, 1)

            def root_sims(n):
                pool.wait_ge(v_q, n + 1)
                pool.tensor_tensor(r1[:, :], q1[:, :], half_m[:, :], ALU.pow).then_inc(g_r, 1)

            def root_x1(n):
                pool.wait_ge(v_q2, n + 1)
                pool.tensor_tensor(r2[:, :], q2[:, :], half_m[:, :], ALU.pow).then_inc(g_r2, 1)

            def low_x(n, r):
                for t in range(2):
                    pool.wait_ge(a_hx, 2 * n + t + 1)
                    pool.tensor_tensor(hl[t][:, 1, :], xb[:, r, t, :], hl[t][:, 0, :], ALU.subtract)\
                        .then_inc(g_lx, 1)

            def scatter(m, t):
                pool.wait_ge(v_mt, m + 1)
                pool.sem_inc(pool_held, 1)
                for c in range(2):
                    pool.indirect_dma_start(
                        out=meta_d, out_offset=bass.IndirectOffsetOnAxis(sli[:, c, t:t + 1], 0),
                        in_=mt[:, t, c, :], in_offset=None).then_inc(d_slots, 16)

            def first_step():
                low_h(0, 0)
                root_sims(1)
                conv_low(1, 0)
                low_h(1, 1)
                conv_low(1, 1)
                root_x1(1)
                conv_low(1, 2)
                low_h(2, 0)
                low_x(1, 1)
                conv_low(1, 3)

            def step(n, r):
                if isinstance(n, int) and n == 1:
                    first_step()
                    return
                U = first_unit(n)
                low_h(U, 1)
                root_sims(n)
                if isinstance(n, int) and n == 2:
                    pool.wait_ge(d_fill, 48)
                scatter(n - 2, 0)
                conv_low(n, 0)
                low_h(U + 1, 0)
                scatter(n - 2, 1)
                conv_low(n, 1)
                low_h(U + 2, 1)
                root_x1(n)
                conv_low(n, 2)
                low_h(U + 3, 0)
                low_x(n, r)
                conv_low(n, 3)

            root_sims(0)
            root_x1(0)
            low_x(0, 0)
            pair_steps(pool, step)

            def gather(s, r):
                pool.wait_ge(d_meta[r], 16 * (s // 2 + 1) if isinstance(s, int) else 8 * (s - r) + 16)
                if not (isinstance(s, int) and s < 2):
                    pool.wait_ge(p_xt, NTILE + s - 1)
                pool.tensor_copy(idxg[:, r:r + 1], meta[:, ds(s, 1), 0:1].rearrange("p a k -> p (a k)"))\
                    .then_inc(g_ig, 1)
                pool.wait_ge(g_ig, s + 1)
                pool.sem_inc(pool_held, 1)
                pool.indirect_dma_start(
                    out=gath[:, r, :, :].rearrange("p s d -> p (s d)"), out_offset=None, in_=hid_d,
                    in_offset=bass.IndirectOffsetOnAxis(idxg[:, r:r + 1], 0)).then_inc(d_gath[r], 16)

            U = first_unit(NPAIR)
            low_h(U, 1)
            scatter(NPAIR - 2, 0)
            scatter(NPAIR - 2, 1)
            low_h(U + 1, 0)
            scatter(NPAIR - 1, 0)
            scatter(NPAIR - 1, 1)
            low_h(U + 2, 1)
            low_h(U + 3, 0)
            pool.wait_ge(p_u, UNITS_SHARED - 4)
            pool.wait_ge(d_hid[0], 16 * NPAIR)
            pool.wait_ge(d_hid[1], 16 * NPAIR)
            gather(0, 0)
            low_h(U + 4, 1)
            gather(1, 1)

            def slot_step(s, r):
                if not (isinstance(s, int) and s == SLOT_TILES):
                    gather(s + 2, r)
                    low_h(UNITS_SHARED + s, r)
                if not (isinstance(s, int) and s == 0):
                    pool.tensor_copy(idxs[:, 1 - r:2 - r], meta[:, ds(s - 1, 1), 0:1].rearrange("p a k -> p (a k)"))\
                        .then_inc(g_is, 1)
                    pool.wait_ge(g_is, s)
                    pool.wait_ge(v_y, NTILE + s)
                    if isinstance(s, int) and s == 1:
                        pool.wait_ge(d_out[0], 16 * NPAIR)
                        pool.wait_ge(d_out[1], 16 * NPAIR)
                    else:
                        pool.wait_ge(d_add, 16 * (s - 1))
                    pool.sem_inc(pool_held, 1)
                    pool.indirect_dma_start(
                        out=out, out_offset=bass.IndirectOffsetOnAxis(idxs[:, 1 - r:2 - r], 0),
                        in_=yb[:, 1 - r, :], in_offset=None, compute_op=ALU.add).then_inc(d_add, 16)

            slot_steps(pool, slot_step)

        @block.scalar
        def _(act):
            def prep_kv(b):
                if b == 0:
                    act.wait_ge(d_bk, 16)
                act.wait_ge(p_kv, b + 1)
                act.activation(kvc_t[:, b, :], prep_ps[b][:, :], ACT.Identity, bias=bk_sb[:, 0:1],
                               accum_out=ksum[:, b:b + 1]).then_inc(a_kv, 1)

            def prep_kc(b):
                act.wait_ge(p_kt, b + 1)
                if b >= 2:
                    act.wait_ge(p_ot, b - 1)
                act.activation(kvc[b % 2].rearrange("p c d -> p (c d)"), prep_ps[b][:, :], ACT.Copy).then_inc(a_kc, 1)

            def prep_ot(b):
                act.wait_ge(p_ot, b + 1)
                act.activation(out_t[:, b, :], prep_ps[b][:, :], ACT.Copy).then_inc(a_ot, 1)

            def columns(n, r):
                act.wait_ge(a_ot, n // 2 + 1 if isinstance(n, int) else B)
                if not (isinstance(n, int) and n == 0):
                    act.wait_ge(p_sim, 2 * n)
                cols = out_t[:, n // 2, :] if isinstance(n, int) else \
                    out_t[:, ds((n - r) // 2, 1), :].rearrange("p a i -> p (a i)")
                act.activation(outs.rearrange("p t i -> p (t i)"), cols[:, 2 * P * r:2 * P * (r + 1)],
                               ACT.Copy).then_inc(a_os, 1)

            def exp_sims(n):
                act.wait_ge(v_nm, n + 1)
                for t in range(2):
                    act.activation(nb[:, t, :], nb[:, t, :], ACT.Exp, bias=ntop[:, t:t + 1],
                                   accum_out=esum[:, t:t + 1]).then_inc(a_exp, 1)

            def exp_router(m):
                act.wait_ge(v_nl, m + 1)
                for t in range(2):
                    act.activation(es[:, t, :], s8[:, t, :], ACT.Exp, bias=nl[:, t:t + 1], scale=1.0 / WSCALE,
                                   accum_out=ez[:, t:t + 1]).then_inc(a_es, 1)

            def norm(n, r):
                act.wait_ge(v_ln, n + 1)
                for t in range(2):
                    act.activation(xb[:, r, t, :], nb[:, t, :], ACT.Identity, bias=nmr[:, t:t + 1],
                                   scale=r2[:, t:t + 1]).then_inc(a_h, 1)
                    act.wait_ge(a_h, 2 * n + t + 1)
                    if not (isinstance(n, int) and n == 0):
                        act.wait_ge(p_xt, 2 * n - 1 + t)
                        act.wait_ge(d_hid[t], 16 * n)
                    act.activation(hl[t][:, 0, :], xb[:, r, t, :], ACT.Copy).then_inc(a_hx, 1)

            def shared_high(c):
                act.wait_ge(d_ws[c // 2], 16)
                act.activation(ws[:, c // QUARTERS, 0, (c % QUARTERS) * CHUNK:(c % QUARTERS + 1) * CHUNK],
                               stage_s[:, c, :], ACT.Copy, scale=WSCALE).then_inc(a_wh, 1)

            def conv(n, u):
                c = 4 * (n - 1) + u
                act.wait_ge(d_st[u % 2], 16 * (2 * (n - 1) + u // 2 + 1))
                if u == 0 and isinstance(n, int):
                    if n == 2:
                        act.wait_ge(v_wl, SHARED_CHUNKS)
                    if n == NPAIR - 1:
                        act.wait_ge(p_sim, 2 * NPAIR)
                        act.wait_ge(a_os, NPAIR)
                        act.wait_ge(g_lx, 2 * (NPAIR - 1))
                    if n == NPAIR:
                        act.wait_ge(p_xt, NTILE)
                        act.wait_ge(g_lx, NTILE)
                        act.wait_ge(d_hid[0], 16 * NPAIR)
                        for t in range(2):
                            act.wait_ge(d_x1w[t], 16 * NPAIR)
                w = wr[:, ds(n - 1, 1), :, :].rearrange("p a s n -> p (a s) n")
                high = w[:, 0, u * CHUNK:(u + 1) * CHUNK]
                last = isinstance(n, int) and n == NPAIR
                if not last:
                    act.activation(stage[:, u % 2, :], stage[:, u % 2, :], ACT.Copy, scale=WSCALE).then_inc(a_cs, 1)
                if not (isinstance(n, int) and c in (0, EXPERT_CHUNKS - 1)):
                    if last and u > 0:
                        act.wait_ge(v_cl, u)
                    else:
                        act.wait_ge(g_cl, c)
                    act.dma_start(stage[:, (u + 1) % 2, :],
                                  wsrc[ds(SHARED_CHUNKS + c + 1, 1)].rearrange("a p n -> p (a n)"))\
                       .then_inc(d_st[(u + 1) % 2], 16)
                if last:
                    act.activation(high, stage[:, u % 2, :], ACT.Copy, scale=WSCALE).then_inc(a_ch, 1)
                else:
                    act.wait_ge(a_cs, c + 1)
                    act.activation(high, stage[:, u % 2, :], ACT.Copy).then_inc(a_ch, 1)

            def mlp_tanh(U, p):
                act.wait_ge(p_g, U + 1)
                act.activation(act_h[:, p, :], g_ps[:, 0:F], ACT.Tanh, scale=0.5 / WSCALE).then_inc(a_th, 1)

            def mlp_high(U, p):
                act.wait_ge(v_h, U + 1)
                act.activation(act_hl[:, p, 0, 0:F], act_h[:, p, :], ACT.Copy).then_inc(a_hi, 1)

            def mlp_act(U, p):
                mlp_tanh(U, p)
                mlp_high(U, p)

            def first_step():
                mlp_act(0, 0)
                prep_ot(3)
                conv(1, 0)
                mlp_tanh(1, 1)
                exp_sims(1)
                mlp_high(1, 1)
                columns(2, 0)
                conv(1, 1)
                exp_router(0)
                mlp_tanh(2, 0)
                conv(1, 2)
                mlp_high(2, 0)
                norm(1, 1)
                conv(1, 3)

            def step(n, r):
                if isinstance(n, int) and n == 1:
                    first_step()
                    return
                U = first_unit(n)
                mlp_act(U, 1)
                conv(n, 0)
                mlp_act(U + 1, 0)
                exp_sims(n)
                conv(n, 1)
                if not (isinstance(n, int) and n == NPAIR - 1):
                    columns(n + 1, 1 - r)
                mlp_act(U + 2, 1)
                exp_router(n - 1)
                conv(n, 2)
                mlp_act(U + 3, 0)
                norm(n, r)
                conv(n, 3)

            act.wait_ge(g_const, 11)
            act.activation(table[:, :], half_m[:, :], ACT.Tanh).then_inc(a_table, 1)
            prep_kv(0)
            prep_kc(0)
            act.wait_ge(d_gates, 16)
            act.activation(tg[:, :], g_sb[:, :], ACT.Tanh).then_inc(a_tg, 1)
            prep_ot(0)
            columns(0, 0)
            prep_kv(1)
            prep_kc(1)
            prep_kv(2)
            for c in range(2):
                shared_high(c)
            exp_sims(0)
            columns(1, 1)
            prep_kc(2)
            prep_ot(1)
            for c in range(2, 5):
                shared_high(c)
            norm(0, 0)
            prep_ot(2)
            prep_kv(3)
            shared_high(5)
            prep_kc(3)
            shared_high(6)
            shared_high(7)
            for c in range(2):
                act.dma_start(stage[:, c, :], wsrc[SHARED_CHUNKS + c]).then_inc(d_st[c], 16)
            pair_steps(act, step)
            U = first_unit(NPAIR)
            mlp_act(U, 1)
            conv(NPAIR, 0)
            exp_router(NPAIR - 1)
            mlp_act(U + 1, 0)
            conv(NPAIR, 1)
            mlp_act(U + 2, 1)
            conv(NPAIR, 2)
            mlp_act(U + 3, 0)
            conv(NPAIR, 3)
            mlp_act(U + 4, 1)

            def slot_step(s, r):
                if not (isinstance(s, int) and s == SLOT_TILES):
                    mlp_act(UNITS_SHARED + s, r)
                if isinstance(s, int) and s == 0:
                    act.wait_ge(v_y, NTILE)
                    act.dma_start(out_tiles[NTILE - 1], yb[:, 1, :]).then_inc(d_out[1], 16)

            slot_steps(act, slot_step)

        @block.vector
        def _(dve):
            chain = {"base": 0, "n": 0}

            def tick(ins):
                chain["n"] += 1
                ins.then_inc(v_chain, 1)

            def settle():
                dve.wait_ge(v_chain, chain["base"] + chain["n"])

            def held():
                dve.sem_inc(dve_held, 1)

            dve.memset(zero, 0.0).then_inc(v_chain, 1)
            chain["n"] += 1
            dve.wait_ge(g_const, 11)
            tick(dve.tensor_copy(iota8[:, :, :], i8[:, :, :]))
            tick(dve.tensor_copy(tok[:, :], sli[:, 0, :]))
            tick(dve.tensor_copy(iota_s[:, :], te[:, :]))
            tick(dve.tensor_scalar(filla, filla, P - 1, None, ALU.bitwise_and))
            settle()
            tick(dve.tensor_scalar(first_slot[:, :, :], iota8[:, :, :], float(T), None, ALU.mult))
            dve.tensor_scalar(fill[:, :, 0], filla, float(T), None, ALU.add).then_inc(v_const, 1)

            def center(b):
                dve.wait_ge(a_kv, b + 1)
                tick(dve.tensor_scalar(kmean[:, b:b + 1], ksum[:, b:b + 1], -1.0 / I, None, ALU.mult))
                settle()
                dve.tensor_scalar(kvc_t[:, b, :], kvc_t[:, b, :], kmean[:, b:b + 1], None, ALU.add).then_inc(v_kc, 1)

            def router_weights():
                dve.wait_ge(d_gw, 16)
                tick(dve.tensor_scalar(gwhl[:, 0, :, :], gw[:, :, :], WSCALE, None, ALU.mult))
                settle()
                dve.scalar_tensor_tensor(gwhl[:, 1, :, :].rearrange("p c e -> p (c e)"),
                                         gw[:, :, :].rearrange("p c e -> p (c e)"), WSCALE,
                                         gwhl[:, 0, :, :].rearrange("p c e -> p (c e)"),
                                         ALU.mult, ALU.subtract).then_inc(v_gw, 1)

            def shared_low(c):
                dve.wait_ge(a_wh, c + 1)
                w = ws[:, c // QUARTERS, :, (c % QUARTERS) * CHUNK:(c % QUARTERS + 1) * CHUNK]
                dve.scalar_tensor_tensor(w[:, 1, :], stage_s[:, c, :], WSCALE, w[:, 0, :],
                                         ALU.mult, ALU.subtract).then_inc(v_wl, 1)

            def last_low(u):
                dve.wait_ge(a_ch, EXPERT_CHUNKS - QUARTERS + u + 1)
                w = wr[:, E - 1, :, u * CHUNK:(u + 1) * CHUNK]
                dve.scalar_tensor_tensor(w[:, 1, :], stage[:, u % 2, :], WSCALE, w[:, 0, :],
                                         ALU.mult, ALU.subtract).then_inc(v_cl, 1)

            def mlp_hidden(U, p):
                dve.wait_ge(a_th, U + 1)
                tick(dve.scalar_tensor_tensor(act_h[:, p, :], act_h[:, p, :], 1.0, g_ps[:, 0:F], ALU.add, ALU.mult))
                settle()
                dve.wait_ge(p_u, U + 1)
                dve.scalar_tensor_tensor(act_h[:, p, :], act_h[:, p, :], 0.5 / WSCALE ** 2, u_ps[:, 0:F],
                                         ALU.mult, ALU.mult).then_inc(v_h, 1)

            def hidden_out(U, p):
                dve.wait_ge(p_ht, U + 1)
                dve.tensor_copy(act_t[:, p, :, :, :], ht_v).then_inc(v_ht, 1)

            def shared_out(m, t):
                dve.wait_ge(p_d, 4 * m + 2 * t + 2)
                dve.wait_ge(d_x1r[t], 16 * (m + 1))
                dve.scalar_tensor_tensor(yb[:, t, :], d_ps[:, :], tgs[:, 0:1], yb[:, t, :], ALU.mult, ALU.add)\
                   .then_inc(v_y, 1)

            def tokens_out(m, t, slot):
                dve.wait_ge(p_xt, 2 * m + t + 1)
                dve.tensor_copy(ring[:, slot, t, :, :, :], xt_ps[:, :, :, :]).then_inc(v_xt, 1)

            def attention_stats(n, r):
                dve.wait_ge(d_x[r], 16 * (n // 2 + 1) if isinstance(n, int) else 8 * (n - r) + 16)
                for t in range(2):
                    tick(dve.bn_stats(stx[:, t, :], xb[:, r, t, :]))
                for t in range(2):
                    dve.wait_ge(p_sim, 2 * n + t + 1)
                    tick(dve.bn_stats(sts[:, t, :], sim_ps[:, t, :]))

            def attention_scale():
                settle()
                held()
                for t in range(2):
                    tick(dve.bn_aggr(mvx[:, t, :], stx[:, t, :]))
                    tick(dve.bn_aggr(mvs[:, t, :], sts[:, t, :]))
                settle()
                tick(dve.tensor_scalar(q1a[:, :], mvx[:, :, 1], LN_EPS, SIM_EPS * H, ALU.add, ALU.mult))
                settle()
                dve.tensor_tensor(q1[:, :], q1a[:, :], mvs[:, :, 1], ALU.add).then_inc(v_q, 1)

            def attention_logits(n):
                dve.wait_ge(g_r, n + 1)
                if isinstance(n, int) and n == 0:
                    dve.wait_ge(d_gb, 32)
                for t in range(2):
                    if not (isinstance(n, int) and n == 0):
                        dve.wait_ge(d_x1w[t], 16 * n)
                    dve.scalar_tensor_tensor(nb[:, t, :], sim_ps[:, t, :], r1[:, t:t + 1], gamma_b,
                                             ALU.mult, ALU.mult).then_inc(v_n, 1)
                for t in range(2):
                    dve.wait_ge(v_n, 2 * n + t + 1)
                    held()
                    tick(dve.tensor_tensor_reduce(out=nb[:, t, :], in0=nb[:, t, :], in1=beta_b, scale=1.0,
                                                  scalar=-3.0e38, op0=ALU.add, op1=ALU.max,
                                                  accum_out=top[:, t:t + 1]))
                settle()
                dve.tensor_scalar(ntop[:, :], top[:, :], -1.0, None, ALU.mult).then_inc(v_nm, 1)

            def attention_add(n, r):
                dve.wait_ge(a_exp, 2 * n + 2)
                tick(dve.reciprocal(rsum[:, :], esum[:, :]))
                settle()
                tick(dve.tensor_scalar(coef[:, :], rsum[:, :], tg[:, 0:1], None, ALU.mult))
                settle()
                for t in range(2):
                    dve.scalar_tensor_tensor(nb[:, t, :], nb[:, t, :], coef[:, t:t + 1], xb[:, r, t, :],
                                             ALU.mult, ALU.add).then_inc(v_x1, 1)
                for t in range(2):
                    dve.wait_ge(v_x1, 2 * n + t + 1)
                    tick(dve.bn_stats(st1[:, t, :], nb[:, t, :]))
                settle()
                held()
                for t in range(2):
                    tick(dve.bn_aggr(mv1[:, t, :], st1[:, t, :]))
                settle()
                dve.tensor_scalar(q2[:, :], mv1[:, :, 1], LN_EPS, None, ALU.add).then_inc(v_q2, 1)

            def attention_norm(n):
                dve.wait_ge(g_r2, n + 1)
                dve.scalar_tensor_tensor(nmr[:, :], mv1[:, :, 0], -1.0, r2[:, :], ALU.mult, ALU.mult).then_inc(v_ln, 1)

            def route_choose(m):
                dve.wait_ge(p_lg, m + 1)
                dve.tensor_copy(lg[:, :, :].rearrange("p t e -> p (t e)"), lg_ps).then_inc(v_lg, 1)
                dve.wait_ge(v_lg, m + 1)
                held()
                for t in range(2):
                    tick(dve.max(s8[:, t, :], lg[:, t, :]))
                settle()
                held()
                for t in range(2):
                    tick(dve.max_index(i8[:, t, :], s8[:, t, :], lg[:, t, :]))
                dve.tensor_scalar(nl[:, :], s8[:, :, 0], -1.0 / WSCALE, None, ALU.mult).then_inc(v_nl, 1)
                settle()
                tick(dve.tensor_copy(idxf[:, :, :], i8[:, :, 0:2]))
                settle()
                for c in range(2):
                    tick(dve.tensor_tensor(mask[:, c, :, :], iota8[:, :, :],
                                           idxf[:, :, c:c + 1].broadcast_to((P, 2, E)), ALU.is_equal))
                settle()
                tick(dve.tensor_tensor(both[:, :, :], mask[:, 0, :, :], mask[:, 1, :, :], ALU.add))
                settle()
                tick(dve.tensor_tensor(before[:, 1, :], before[:, 0, :], both[:, 0, :], ALU.add))
                settle()
                dve.tensor_tensor(before[:, 2, :], before[:, 1, :], both[:, 1, :], ALU.add).then_inc(v_m, 1)

            def route_place(m):
                dve.wait_ge(p_rk, m + 1)
                dve.tensor_tensor(rk[:, :, :].rearrange("p t e -> p (t e)"), rk_ps,
                                  first_slot[:, :, :].rearrange("p t e -> p (t e)"), ALU.add).then_inc(v_rk, 1)
                dve.wait_ge(v_m, m + 1)
                tick(dve.tensor_copy(before[:, 0, :], before[:, 2, :]))
                dve.wait_ge(a_es, 2 * m + 2)
                tick(dve.reciprocal(rz[:, :], ez[:, :]))
                dve.wait_ge(v_rk, m + 1)
                for c in range(2):
                    tick(dve.tensor_tensor(rkm[:, c, :, :], mask[:, c, :, :], rk[:, :, :], ALU.mult))
                settle()
                tick(dve.tensor_reduce(slf[:, :, :].rearrange("p c t -> p (c t)"),
                                       rkm[:, :, :, :].rearrange("p c t e -> p (c t) e"), AX.X, ALU.add))
                tick(dve.tensor_tensor(p12[:, :, :], es[:, :, 0:2], rz[:, :].unsqueeze(2).broadcast_to((P, 2, 2)),
                                       ALU.mult))
                settle()
                if not (isinstance(m, int) and m == 0):
                    dve.wait_ge(d_slots, 64 * m)
                tick(dve.tensor_copy(sli[:, :, :], slf[:, :, :]))
                tick(dve.tensor_reduce(psm[:, :], p12[:, :, :], AX.X, ALU.add))
                settle()
                tick(dve.tensor_scalar(pse[:, :], psm[:, :], 1e-20, None, ALU.add))
                settle()
                tick(dve.reciprocal(prs[:, :], pse[:, :]))
                settle()
                tick(dve.tensor_tensor(mt[:, :, :, 1].bitcast(fp32), p12[:, :, :],
                                       prs[:, :].unsqueeze(2).broadcast_to((P, 2, 2)), ALU.mult))
                for t in range(2):
                    tick(dve.tensor_copy(mt[:, t, :, 0], tok[:, t:t + 1].broadcast_to((P, 2))))
                settle()
                dve.tensor_scalar(tok[:, :], tok[:, :], float(2 * P), None, ALU.add).then_inc(v_mt, 1)

            def slot_tables():
                tick(dve.tensor_scalar(cnt[:, 0, :], tot_ps[0:1, :], float(P - 1), None, ALU.add))
                settle()
                tick(dve.tensor_scalar(cnt[:, 1, :], cnt[:, 0, :], P.bit_length() - 1, None, ALU.arith_shift_right))
                settle()
                tick(dve.tensor_copy(ends[:, 0, :], cnt[:, 1, :]))
                settle()
                for i in range(3):
                    d = 1 << i
                    tick(dve.tensor_copy(ends[:, i + 1, 0:d], ends[:, i, 0:d]))
                    tick(dve.tensor_tensor(ends[:, i + 1, d:E], ends[:, i, d:E], ends[:, i, 0:E - d], ALU.add))
                    settle()
                ends_b = ends[:, 3:4, :].broadcast_to((1, TABLE, E))
                tick(dve.tensor_tensor(past, iota_s[:, :].unsqueeze(2).broadcast_to((1, TABLE, E)), ends_b, ALU.is_ge))
                settle()
                tick(dve.tensor_tensor(past_end, past, ends_b, ALU.mult))
                tick(dve.tensor_reduce(tab[:, 0, :], past, AX.X, ALU.add))
                settle()
                tick(dve.tensor_reduce(tab[:, 1, :], past_end, AX.X, ALU.max))
                settle()
                tick(dve.tensor_scalar(te[:, :], tab[:, 0, :], float(E - 1), None, ALU.min))
                tick(dve.tensor_tensor(tab[:, 2, :], iota_s[:, :], tab[:, 1, :], ALU.subtract))
                settle()
                tick(dve.tensor_scalar(tab[:, 2, :], tab[:, 2, :], float(P), None, ALU.mult))
                settle()
                dve.scalar_tensor_tensor(tr[:, :], tab[:, 0, :], float(T), tab[:, 2, :], ALU.mult, ALU.add)\
                   .then_inc(v_tab, 1)

            def first_step():
                tokens_out(0, 0, 0)
                center(3)
                tokens_out(0, 1, 0)
                for c in range(5, SHARED_CHUNKS):
                    shared_low(c)
                mlp_hidden(0, 0)
                router_weights()
                attention_stats(1, 1)
                attention_scale()
                attention_logits(1)
                hidden_out(0, 0)
                mlp_hidden(1, 1)
                route_choose(0)
                attention_add(1, 1)
                hidden_out(1, 1)
                mlp_hidden(2, 0)
                attention_norm(1)
                route_place(0)
                shared_out(0, 0)

            def step(n, r):
                if isinstance(n, int) and n == 1:
                    first_step()
                    return
                U = first_unit(n)
                attention_stats(n, r)
                hidden_out(U - 1, 0)
                tokens_out(n - 1, 0, 1 - r)
                mlp_hidden(U, 1)
                tokens_out(n - 1, 1, 1 - r)
                attention_scale()
                hidden_out(U, 1)
                mlp_hidden(U + 1, 0)
                attention_logits(n)
                shared_out(n - 2, 1)
                route_choose(n - 1)
                hidden_out(U + 1, 0)
                mlp_hidden(U + 2, 1)
                attention_add(n, r)
                hidden_out(U + 2, 1)
                mlp_hidden(U + 3, 0)
                attention_norm(n)
                route_place(n - 1)
                shared_out(n - 1, 0)

            center(0)
            attention_stats(0, 0)
            center(1)
            attention_scale()
            attention_logits(0)
            center(2)
            shared_low(0)
            shared_low(1)
            dve.wait_ge(a_tg, 1)
            tick(dve.tensor_scalar(tgs[:, :], tg[:, 1:2], 1.0 / WSCALE, None, ALU.mult))
            attention_add(0, 0)
            shared_low(2)
            attention_norm(0)
            for c in range(3, 5):
                shared_low(c)

            STEP_TICKS = 43
            step(1, 1)
            step(2, 0)
            before_loop = chain["n"]
            with dve.Fori(1, NPAIR // 2 - 1) as k:
                chain["base"], chain["n"] = before_loop + (k - 1) * (2 * STEP_TICKS), 0
                step(2 * k + 1, 1)
                step(2 * k + 2, 0)
                assert chain["n"] == 2 * STEP_TICKS, chain["n"]
            chain["base"], chain["n"] = 0, before_loop + (NPAIR // 2 - 2) * 2 * STEP_TICKS
            step(NPAIR - 1, 1)

            U = first_unit(NPAIR)
            hidden_out(U - 1, 0)
            tokens_out(NPAIR - 1, 0, 1)
            mlp_hidden(U, 1)
            tokens_out(NPAIR - 1, 1, 1)
            hidden_out(U, 1)
            route_choose(NPAIR - 1)
            mlp_hidden(U + 1, 0)
            last_low(0)
            shared_out(NPAIR - 2, 1)
            route_place(NPAIR - 1)
            hidden_out(U + 1, 0)
            mlp_hidden(U + 2, 1)
            last_low(1)
            slot_tables()
            hidden_out(U + 2, 1)
            mlp_hidden(U + 3, 0)
            last_low(2)
            shared_out(NPAIR - 1, 0)
            last_low(3)
            hidden_out(U + 3, 0)
            mlp_hidden(U + 4, 1)

            def slot_tokens_out(s, r):
                dve.wait_ge(p_xt, NTILE + s + 1)
                dve.tensor_copy(xg_t[:, r, :, :, :], xt_ps[:, :, :, :]).then_inc(v_xt, 1)

            def slot_step(s, r):
                U = UNITS_SHARED + s
                hidden_out(U - 1, 1 - r)
                if not (isinstance(s, int) and s == SLOT_TILES):
                    slot_tokens_out(s + 1, 1 - r)
                    mlp_hidden(U, r)
                if isinstance(s, int) and s == 0:
                    shared_out(NPAIR - 1, 1)
                    return
                dve.wait_ge(p_d, U)
                if isinstance(s, int) and s < 3:
                    dve.wait_ge(d_out[s - 1], 16 * NPAIR)
                else:
                    dve.wait_ge(d_add, 16 * (s - 2))
                w = meta[:, ds(s - 1, 1), 1:2].rearrange("p a k -> p (a k)").bitcast(fp32)
                dve.tensor_scalar(yb[:, 1 - r, :], d_ps[:, :], w, tgs[:, 0:1], ALU.mult, ALU.mult).then_inc(v_y, 1)

            slot_tokens_out(0, 0)
            head = chain["n"]
            for s in range(3):
                slot_step(s, s % 2)
            assert chain["n"] == head + 3
            with dve.Fori(1, SLOT_TILES // 2) as k:
                chain["base"], chain["n"] = head + 3 + (k - 1) * 2, 0
                slot_step(2 * k + 1, 1)
                slot_step(2 * k + 2, 0)
            chain["base"], chain["n"] = 0, head + 3 + (SLOT_TILES // 2 - 1) * 2
            slot_step(SLOT_TILES, 1)

        @block.tensor
        def _(pe):
            PRODUCTS = ((0, 0), (0, 1), (1, 0))
            UP_FIRST = 1

            def prep_kv(b):
                pe.wait_ge(d_ctx[b], 16)
                pe.matmul(prep_ps[b][:, :], wk_sb, ctx_t[:, b, :], start=True, stop=True).then_inc(p_kv, 1)

            def prep_kc(b):
                pe.wait_ge(v_kc, b + 1)
                for c in range(HC):
                    mm = pe.transpose(prep_ps[b][:, c * P:(c + 1) * P], kvc_t[:, b, c * P:(c + 1) * P], id32)
                mm.then_inc(p_kt, 1)

            def prep_ot(b):
                pe.wait_ge(a_kc, b + 1)
                pe.wait_ge(d_xt[b], 16)
                for c in range(HC):
                    mm = pe.matmul(prep_ps[b][:, :], kvc[b % 2][:, c, :], x_t[:, b, c, :], start=(c == 0), stop=(c == HC - 1))
                mm.then_inc(p_ot, 1)

            def sims(n, r):
                pe.wait_ge(a_os, n + 1)
                kv = kvc_t[:, n // 2, :] if isinstance(n, int) else \
                    kvc_t[:, ds((n - r) // 2, 1), :].rearrange("p a i -> p (a i)")
                for t in range(2):
                    if not (isinstance(n, int) and n == 0):
                        pe.wait_ge(v_n, 2 * n - 1 + t)
                    pe.matmul(sim_ps[:, t, :], outs[:, t, :], kv, start=True, stop=True).then_inc(p_sim, 1)

            def transpose_tokens(src):
                for h in range(2):
                    for c in range(HC):
                        mm = pe.transpose(xt_ps[:, h, c, :], src[:, h, c * P:(c + 1) * P], id16[:, :])
                mm.then_inc(p_xt, 1)

            def pair_tokens(m, t):
                pe.wait_ge(g_lx, 2 * m + t + 1)
                if not (isinstance(m, int) and m == 0 and t == 0):
                    pe.wait_ge(v_xt, 2 * m + t)
                transpose_tokens(hl[t])

            def router_logits(m, slot):
                pe.wait_ge(v_xt, 2 * m + 2)
                if isinstance(m, int) and m == 0:
                    pe.wait_ge(v_gw, 1)
                else:
                    pe.wait_ge(v_rk, m)
                for t in range(2):
                    for c in range(HC):
                        for i, (a, b) in enumerate(PRODUCTS):
                            mm = pe.matmul(lg_ps[:, t * E:(t + 1) * E], ring[:, slot, t, a, c, :], gwhl[:, b, c, :],
                                           start=(c == 0 and i == 0), stop=(c == HC - 1 and i == 2))
                mm.then_inc(p_lg, 1)

            def router_ranks(m):
                pe.wait_ge(v_m, m + 1)
                pe.matmul(rk_ps, below[:, :], both[:, :, :].rearrange("p t e -> p (t e)"), start=True, stop=False)
                mm = pe.matmul(rk_ps, ones[:, :], before[:, 0:2, :].rearrange("p t e -> p (t e)"), start=False, stop=True)
                if isinstance(m, int) and m == NPAIR - 1:
                    mm = pe.matmul(tot_ps, ones[:, :], before[:, 2, :], start=True, stop=True)
                mm.then_inc(p_rk, 1)

            def up_or_gate(ps, at, xs, w, chunks=range(HC)):
                for c in chunks:
                    for i, (a, b) in enumerate(PRODUCTS):
                        mm = pe.matmul(ps[:, 0:F], xs[:, a, c, :], w[:, b, at + c * F:at + (c + 1) * F],
                                       start=(c == 0 and i == 0), stop=(c == HC - 1 and i == 2))
                return mm

            def gate(xs, w):
                up_or_gate(g_ps, GATE, xs, w).then_inc(p_g, 1)

            def up_first(xs, w):
                up_or_gate(u_ps, UP, xs, w, range(UP_FIRST))

            def up_rest(xs, w):
                up_or_gate(u_ps, UP, xs, w, range(UP_FIRST, HC)).then_inc(p_u, 1)

            def transpose_hidden(U, p):
                pe.wait_ge(g_lh, U + 1)
                for h in range(2):
                    for c in range(FC):
                        mm = pe.transpose(ht_v[:, h, c, :], act_hl[:, p, h, c * P:(c + 1) * P], id16[:, :])
                mm.then_inc(p_ht, 1)

            def down(U, p, w, first, last):
                pe.wait_ge(v_ht, U + 1)
                for c in range(FC):
                    for i, (a, b) in enumerate(PRODUCTS):
                        mm = pe.matmul(d_ps[:, :], act_t[:, p, a, c, :], w[:, b, DOWN + c * H:DOWN + (c + 1) * H],
                                       start=(first and c == 0 and i == 0), stop=(last and c == FC - 1 and i == 2))
                mm.then_inc(p_d, 1)

            def unit(n, r, j, between=None, after=None):
                U, p = first_unit(n) + j, (j + 1) % 2
                xs = ring[:, r, 1, :, :, :] if j == 0 else ring[:, 1 - r, j // 3, :, :, :]
                w, w_before = ws[:, p, :, :], ws[:, 1 - p, :, :]
                if j in (1, 3):
                    pe.wait_ge(v_xt, 2 * (n - 1) + j // 3 + 1)
                if isinstance(n, int) and n == 1 and j < 3:
                    pe.wait_ge(v_wl, j * QUARTERS)
                    pe.wait_ge(a_ot, 3)
                piped = not (isinstance(n, int) and n == 1 and j == 1)
                if piped:
                    pe.wait_ge(v_h, U)
                gate(xs, w)
                up_first(xs, w)
                if piped:
                    transpose_hidden(U - 1, 1 - p)
                if between:
                    between()
                up_rest(xs, w)
                if after:
                    after()
                if piped:
                    if p == 1 and not (isinstance(n, int) and n == 1):
                        pe.wait_ge(v_y, 2 * n - 3 + j // 2)
                    if isinstance(n, int) and n == 1 and j == 2:
                        pe.wait_ge(a_ot, B)
                    down(U - 1, 1 - p, w_before, p == 1, p == 0)

            def first_step():
                pair_tokens(0, 0)
                pair_tokens(0, 1)
                prep_kc(3)
                unit(1, 1, 1)
                prep_ot(3)
                router_logits(0, 0)
                unit(1, 1, 2)
                unit(1, 1, 3, lambda: router_ranks(0))
                sims(2, 0)

            def step(n, r):
                if isinstance(n, int) and n == 1:
                    first_step()
                    return
                m = n - 1
                unit(n, r, 0, lambda: pair_tokens(m, 0), lambda: pair_tokens(m, 1))
                unit(n, r, 1)
                router_logits(m, 1 - r)
                unit(n, r, 2)
                router_ranks(m)
                unit(n, r, 3)
                if not (isinstance(n, int) and n == NPAIR - 1):
                    sims(n + 1, 1 - r)

            pe.wait_ge(g_const, 11)
            pe.wait_ge(d_wk, 16)
            prep_kv(0)
            prep_kc(0)
            prep_ot(0)
            prep_kv(1)
            sims(0, 0)
            prep_kv(2)
            prep_kc(1)
            prep_ot(1)
            prep_kc(2)
            sims(1, 1)
            prep_ot(2)
            prep_kv(3)
            pair_steps(pe, step)

            def expert(s):
                e = pe.value_load(te[0:1, ds(s, 1)], min_val=0, max_val=E - 1)
                return wr[:, ds(e, 1), :, :].rearrange("p a s n -> p (a s) n")

            def slot_tokens(s, r):
                pe.wait_ge(d_gath[r], 16 * (s // 2 + 1) if isinstance(s, int) else 8 * (s - r) + 16)
                pe.wait_ge(v_xt, NTILE + s)
                transpose_tokens(gath[:, r, :, :])

            unit(NPAIR, 0, 0, lambda: pair_tokens(NPAIR - 1, 0), lambda: pair_tokens(NPAIR - 1, 1))
            router_logits(NPAIR - 1, 1)
            unit(NPAIR, 0, 1)
            router_ranks(NPAIR - 1)
            unit(NPAIR, 0, 2)
            unit(NPAIR, 0, 3)
            unit(NPAIR + 1, 1, 0, None, lambda: slot_tokens(0, 0))
            pe.wait_ge(v_tab, 1)
            pe.wait_ge(g_cl, EXPERT_CHUNKS - QUARTERS)
            pe.wait_ge(v_cl, QUARTERS)

            def slot_step(s, r):
                U = UNITS_SHARED + s
                last, first = isinstance(s, int) and s == SLOT_TILES, isinstance(s, int) and s == 0
                if not last:
                    w = expert(s)
                    pe.wait_ge(v_xt, NTILE + s + 1)
                    pe.wait_ge(v_h, U)
                    gate(xg_t[:, r, :, :, :], w)
                    up_first(xg_t[:, r, :, :, :], w)
                transpose_hidden(U - 1, 1 - r)
                if not last:
                    slot_tokens(s + 1, 1 - r)
                    up_rest(xg_t[:, r, :, :, :], w)
                if first:
                    down(U - 1, 1, ws[:, 1, :, :], False, True)
                else:
                    w = expert(s - 1)
                    pe.wait_ge(v_y, NTILE + s - 1)
                    down(U - 1, 1 - r, w, True, True)

            slot_steps(pe, slot_step)


_OUTS = [((T + P, H), "float32")]


def kernel(**inputs):
    import numpy as np
    import concourse.bacc as bacc
    from concourse.bass_utils import run_bass_kernel_spmd

    a = {k: np.asarray(v) for k, v in inputs.items()}

    def unit(gate, up, down):
        parts = [m.T.reshape(HC, P, F).transpose(1, 0, 2).reshape(P, HC * F) for m in (gate, up)]
        d = np.zeros((FP, H), down.dtype)
        d[0:F] = down.T
        parts.append(d.reshape(FC, P, H).transpose(1, 0, 2).reshape(P, FC * H))
        return np.concatenate(parts, axis=1)

    sg, su, sd = a["L0_ffn_sw_gate"], a["L0_ffn_sw_up"], a["L0_ffn_sw_down"]
    units = [unit(sg[i * F:(i + 1) * F], su[i * F:(i + 1) * F], sd[:, i * F:(i + 1) * F]) for i in range(SHARED_UNITS)]
    units += [unit(a["L0_ffn_w_gate"][e], a["L0_ffn_w_up"][e], a["L0_ffn_w_down"][e]) for e in range(E)]
    wsrc = np.stack(units).reshape(SHARED_UNITS + E, P, QUARTERS, CHUNK).transpose(0, 2, 1, 3).reshape(NCHUNK, P, CHUNK)
    arrays = {
        "x": a["x"].reshape(T, H),
        "xT": a["x"].transpose(0, 2, 1).reshape(B, HC, P, I).transpose(0, 2, 1, 3),
        "ctxT": a["ctx_512"].transpose(2, 0, 1),
        "wkT": a["L0_xattn_W_k"].T,
        "bk": a["L0_xattn_b_k"].reshape(DC, 1),
        "gates": np.concatenate([a["g_xattn"], a["g_ffn"]]),
        "gamma": a["L0_xattn_ln_gamma"],
        "beta": a["L0_xattn_ln_beta"],
        "gwT": a["L0_ffn_gate_weight"].T.reshape(HC, P, E).transpose(1, 0, 2),
        "wsrc": wsrc,
    }
    nc = bacc.Bacc("TRN2", target_bir_lowering=False, num_devices=1)
    args = []
    for name in arrays:
        arrays[name] = np.ascontiguousarray(arrays[name])
        args.append(nc.dram_tensor(name, arrays[name].shape, mybir.dt.from_np(arrays[name].dtype),
                                   kind="ExternalInput").ap())
    shape, dtype = _OUTS[0]
    args.append(nc.dram_tensor("out", shape, mybir.dt.from_np(np.dtype(dtype)), kind="ExternalOutput").ap())
    flamingo_block(nc, *args)
    r = run_bass_kernel_spmd(nc, [arrays], core_ids=[0])
    return r.results[0]["out"][0:T].reshape(B, I, H)
```

```python
import concourse.bass as bass
from concourse import mybir
from contextlib import ExitStack

B, I, H = 4, 512, 512
DC = 128
E, F, TOPK = 8, 352, 2
P = 128
T = B * I
NTILE = T // P
NPAIR = NTILE // 2
HC = H // P
FC = -(-F // P)
FP = FC * P
GATE, UP, DOWN = 0, HC * F, 2 * HC * F
UNIT = DOWN + FC * H
QUARTERS = 4
CHUNK = UNIT // QUARTERS
SHARED_UNITS = 2
SHARED_CHUNKS, EXPERT_CHUNKS = SHARED_UNITS * QUARTERS, E * QUARTERS
NCHUNK = SHARED_CHUNKS + EXPERT_CHUNKS
SLOT_TILES = (T * TOPK + E * (P - 1)) // P
AHEAD = 2
TABLE = SLOT_TILES + AHEAD
META_ROWS = E * T + 10 * P
LN_EPS, SIM_EPS = 1e-5, 1e-6
WSCALE = 256.0


def flamingo_block(nc, x, xT, ctxT, wkT, bk, gates, gamma, beta, gwT, wsrc, out):
    fp32, fp16 = mybir.dt.float32, mybir.dt.float16
    i32, u32 = mybir.dt.int32, mybir.dt.uint32
    ALU, ACT, AX = mybir.AluOpType, mybir.ActivationFunctionType, mybir.AxisListType
    ds = bass.ds

    x1_d = nc.dram_tensor("x1_d", (T, H), fp32, kind="Internal").ap()
    hid_d = nc.dram_tensor("hid_d", (T + P, 2 * H), fp16, kind="Internal").ap()
    meta_d = nc.dram_tensor("meta_d", (META_ROWS, 2), i32, kind="Internal").ap()

    def by_tile(ap):
        return ap[0:T, :].rearrange("(n p) d -> n p d", p=P)

    x_pairs = x.rearrange("(n t p) d -> n p t d", t=2, p=P)
    x1_tiles, hid_tiles, out_tiles = by_tile(x1_d), by_tile(hid_d), by_tile(out)

    ctx = ExitStack()
    with ctx:
        def sb(name, shape, dt):
            return ctx.enter_context(nc.sbuf_tensor(name, shape, dt))

        def pb(name, shape, dt):
            return ctx.enter_context(nc.psum_tensor(name, shape, dt))

        def sem(name):
            return ctx.enter_context(nc.semaphore(name))

        ws = sb("ws", [P, SHARED_UNITS, 2, UNIT], fp16)
        wr = sb("wr", [P, E, 2, UNIT], fp16)

        def overlay(expert, offset, words, dt=fp32):
            flat = wr[:, :, :, :].rearrange("p e s n -> p (e s n)")
            at = expert * 2 * UNIT + 2 * offset
            v = flat[:, at:at + 2 * words]
            return v if dt == fp16 else v.bitcast(dt)

        ctx_t = overlay(3, 0, B * I).rearrange("p (b i) -> p b i", b=B)
        x_t = overlay(4, 0, B * HC * I).rearrange("p (b c i) -> p b c i", b=B, c=HC)
        kv_keys = [overlay(4, B * HC * I, HC * DC).rearrange("p (c d) -> p c d", c=HC),
                   overlay(3, B * I + 1312, HC * DC).rearrange("p (c d) -> p c d", c=HC)]
        kv_t = overlay(6, 0, B * I).rearrange("p (b i) -> p b i", b=B)
        xkv_t = overlay(6, B * I, B * I).rearrange("p (b i) -> p b i", b=B)
        x_in = overlay(6, 2 * B * I, 4 * H).rearrange("p (r t d) -> p r t d", r=2, t=2)
        x1_buf = overlay(6, 2 * B * I + 4 * H, 2 * H).rearrange("p (t d) -> p t d", t=2)
        gamma_b = overlay(6, 2 * B * I + 6 * H, H)
        beta_b = overlay(6, 2 * B * I + 7 * H, H)
        halves0 = overlay(6, 2 * B * I + 8 * H, H, fp16).rearrange("p (s d) -> p s d", s=2)

        stage_s = overlay(1, 0, SHARED_CHUNKS * CHUNK).rearrange("p (c n) -> p c n", c=SHARED_CHUNKS)
        stage = sb("stage", [P, 2, CHUNK], fp32)
        ring = sb("ring", [P, 2, 2, 2, HC, P], fp16)
        slots_t = sb("slots_t", [P, 2, 2, HC, P], fp16)
        halves1 = slots_t[:, 1, :, :, :].rearrange("p s c n -> p s (c n)")
        pair_cols = slots_t[:, 0, :, :, :].rearrange("p s c n -> p (s c n)").bitcast(fp32)[:, 0:2 * P]\
            .rearrange("p (t i) -> p t i", t=2)
        act_h = sb("act_h", [P, 2, F], fp32)
        act_hl = sb("act_hl", [P, 2, 2, FP], fp16)
        act_t = sb("act_t", [P, 2, 2, FC, P], fp16)
        rows = sb("rows", [P, 2, H], fp32)
        gathered = ring[:, 0, :, :, :, :].rearrange("p t s c n -> p t s (c n)")
        halves = [halves0, halves1]

        id32 = overlay(3, B * I + 1024, P)
        id16 = sb("id16", [P, P], fp16)
        below = sb("below", [P, P], fp16)
        ones = sb("ones", [P, P], fp16)
        wk_sb = overlay(3, B * I + 1152, DC)
        bk_sb = sb("bk_sb", [P, 1], fp32)
        ksum = sb("ksum", [P, B], fp32)
        kmean = sb("kmean", [P, B], fp32)
        gates_in = sb("gates_in", [P, 2], fp32)
        gates_t = sb("gates_t", [P, 2], fp32)
        ffn_gate = sb("ffn_gate", [P, 1], fp32)
        table = sb("table", [P, 2], fp32)
        router_w = overlay(3, B * I + 1280, HC * E).rearrange("p (c e) -> p c e", c=HC)
        router_hl = sb("router_hl", [P, 2, HC, E], fp16)
        half_m = sb("half_m", [P, 2], fp32)
        stats_x = sb("stats_x", [P, 2, 6], fp32)
        stats_sims = sb("stats_sims", [P, 2, 6], fp32)
        stats_x1 = sb("stats_x1", [P, 2, 6], fp32)
        moments_x = sb("moments_x", [P, 2, 2], fp32)
        moments_sims = sb("moments_sims", [P, 2, 2], fp32)
        moments_x1 = sb("moments_x1", [P, 2, 2], fp32)
        x_term = sb("x_term", [P, 2], fp32)
        sims_q = sb("sims_q", [P, 2], fp32)
        sims_r = sb("sims_r", [P, 2], fp32)
        x1_q = sb("x1_q", [P, 2], fp32)
        x1_r = sb("x1_r", [P, 2], fp32)
        x1_shift = sb("x1_shift", [P, 2], fp32)
        sims_max = sb("sims_max", [P, 2], fp32)
        neg_max = sb("neg_max", [P, 2], fp32)
        esum = sb("esum", [P, 2], fp32)
        rsum = sb("rsum", [P, 2], fp32)
        coef = sb("coef", [P, 2], fp32)
        logits = sb("logits", [P, 2, E], fp32)
        top8 = sb("top8", [P, 2, 8], fp32)
        top8_at = sb("top8_at", [P, 2, 8], u32)
        choice = sb("choice", [P, 2, 2], fp32)
        iota8 = sb("iota8", [P, 2, E], fp32)
        mask = sb("mask", [P, 2, 2, E], fp32)
        both = sb("both", [P, 2, E], fp16)
        before = sb("before", [P, 3, E], fp16)
        neg_top = sb("neg_top", [P, 2], fp32)
        top_exp = sb("top_exp", [P, 2, 8], fp32)
        router_sum = sb("router_sum", [P, 2], fp32)
        router_rsum = sb("router_rsum", [P, 2], fp32)
        probs = sb("probs", [P, 2, 2], fp32)
        probs_sum = sb("probs_sum", [P, 2], fp32)
        probs_sum_eps = sb("probs_sum_eps", [P, 2], fp32)
        probs_rsum = sb("probs_rsum", [P, 2], fp32)
        first_slot = sb("first_slot", [P, 2, E], fp32)
        ranks = sb("ranks", [P, 2, E], fp32)
        chosen_rank = sb("chosen_rank", [P, 2, 2, E], fp32)
        slot_f = sb("slot_f", [P, 2, 2], fp32)
        slot_of = sb("slot_of", [P, 2, 2], i32)
        token_id = sb("token_id", [P, 2], fp32)
        slot_entry = sb("slot_entry", [P, 2, 2, 2], i32)
        fill = overlay(3, B * I, 2 * (META_ROWS // P), i32).rearrange("p (c k) -> p c k", k=2)
        filla = overlay(3, B * I + 324, META_ROWS // P, i32)
        zero = overlay(3, B * I + 512, H, fp32)
        meta = sb("meta", [P, TABLE, 2], i32)
        gather_rows = sb("gather_rows", [P, 2], i32)
        add_rows = sb("add_rows", [P, 2], i32)
        tile_count = sb("tile_count", [1, 2, E], i32)
        ends = sb("ends", [1, 4, E], fp32)
        iota_s = sb("iota_s", [1, TABLE], fp32)
        tab = sb("tab", [1, 3, TABLE], fp32)
        tile_expert = sb("tile_expert", [1, TABLE], i32)
        tile_row = sb("tile_row", [1, TABLE], i32)

        misc = pb("misc", [P, 512], fp32)
        sim_ps = pb("sim_ps", [P, 2, 512], fp32)
        g_ps = pb("g_ps", [P, 512], fp32)
        u_ps = pb("u_ps", [P, 512], fp32)
        d_ps = pb("d_ps", [P, 512], fp32)
        xt_ps = pb("xt_ps", [P, 2, HC, P], fp16)
        ht_ps = pb("ht_ps", [P, 1024], fp16)
        ht_v = ht_ps[:, 0:2 * FP].rearrange("p (s c n) -> p s c n", s=2, c=FC)
        logits_ps = misc[:, 0:2 * E]
        ranks_ps = misc[:, 32:32 + 2 * E]
        totals_ps = misc[:, 64:64 + E]
        prep_ps = [misc, g_ps, u_ps, d_ps]
        past = sim_ps[0:1, 0, 0:TABLE * E].rearrange("p (s e) -> p s e", e=E)
        past_end = sim_ps[0:1, 1, 0:TABLE * E].rearrange("p (s e) -> p s e", e=E)

        wk_loaded, bk_loaded, gates_loaded = sem("wk_loaded"), sem("bk_loaded"), sem("gates_loaded")
        gamma_beta_loaded, router_loaded = sem("gamma_beta_loaded"), sem("router_loaded")
        ctx_loaded = [sem(f"ctx_loaded{b}") for b in range(B)]
        xt_loaded = [sem(f"xt_loaded{b}") for b in range(B)]
        shared_loaded = [sem(f"shared_loaded{i}") for i in range(SHARED_CHUNKS // 2)]
        x_loaded = [sem(f"x_loaded{r}") for r in range(2)]
        quarter_loaded = [sem(f"quarter_loaded{r}") for r in range(2)]
        x1_stored = [sem(f"x1_stored{t}") for t in range(2)]
        x1_loaded = [sem(f"x1_loaded{t}") for t in range(2)]
        tokens_stored = [sem(f"tokens_stored{t}") for t in range(2)]
        out_stored = [sem(f"out_stored{t}") for t in range(2)]
        cleared, slots_scattered, rows_added = sem("cleared"), sem("slots_scattered"), sem("rows_added")
        meta_loaded = [sem(f"meta_loaded{r}") for r in range(2)]
        slots_gathered = [sem(f"slots_gathered{r}") for r in range(2)]
        kv_ready, kv_transposed, xkv_ready = sem("kv_ready"), sem("kv_transposed"), sem("xkv_ready")
        first_xkv_ready, sims_ready = sem("first_xkv_ready"), sem("sims_ready")
        tokens_transposed, logits_ready, ranks_ready = sem("tokens_transposed"), sem("logits_ready"), sem("ranks_ready")
        gate_ready, up_ready, down_ready = sem("gate_ready"), sem("up_ready"), sem("down_ready")
        hidden_transposed = sem("hidden_transposed")
        kv_biased, kv_keys_out, xkv_out, columns_out = (
            sem("kv_biased"), sem("kv_keys_out"), sem("xkv_out"), sem("columns_out"))
        gates_tanh, tanh_ready, sims_exp, router_exp = (
            sem("gates_tanh"), sem("tanh_ready"), sem("sims_exp"), sem("router_exp"))
        tokens_normed, tokens_high, hidden_high = sem("tokens_normed"), sem("tokens_high"), sem("hidden_high")
        quarter_scaled, quarter_high, shared_high_made = (
            sem("quarter_scaled"), sem("quarter_high"), sem("shared_high_made"))
        vector_order, fill_ready, router_split = sem("vector_order"), sem("fill_ready"), sem("router_split")
        shared_low_made, last_low_made, kv_centred = sem("shared_low_made"), sem("last_low_made"), sem("kv_centred")
        sims_var_ready, sims_left, max_ready = sem("sims_var_ready"), sem("sims_left"), sem("max_ready")
        x1_ready, x1_var_ready, shift_ready = sem("x1_ready"), sem("x1_var_ready"), sem("shift_ready")
        hidden_ready, hidden_left, tokens_left = sem("hidden_ready"), sem("hidden_left"), sem("tokens_left")
        rows_ready, logits_left, ranks_left = sem("rows_ready"), sem("logits_left"), sem("ranks_left")
        router_max_ready, counts_ready = sem("router_max_ready"), sem("counts_ready")
        slots_ready, tables_ready = sem("slots_ready"), sem("tables_ready")
        pool_order, constants_made = sem("pool_order"), sem("constants_made")
        sims_root, x1_root, hidden_low, tokens_low = sem("sims_root"), sem("x1_root"), sem("hidden_low"), sem("tokens_low")
        quarter_low, gather_rows_ready, add_rows_ready = (
            sem("quarter_low"), sem("gather_rows_ready"), sem("add_rows_ready"))

        dve_held, pool_held, sp_held = sem("dve_held"), sem("pool_held"), sem("sp_held")

        block = ctx.enter_context(nc.Block())

        def pair_steps(eng, step):
            step(1, 1)
            step(2, 0)
            with eng.Fori(1, NPAIR // 2 - 1) as k:
                step(2 * k + 1, 1)
                step(2 * k + 2, 0)
            step(NPAIR - 1, 1)

        def first_unit(n):
            return 4 * (n - 1) - 1

        def slot_steps(eng, step):
            for s in range(3):
                step(s, s % 2)
            with eng.Fori(1, SLOT_TILES // 2) as k:
                step(2 * k + 1, 1)
                step(2 * k + 2, 0)
            step(SLOT_TILES, 1)

        UNITS_SHARED = NTILE * SHARED_UNITS

        @block.sync
        def _(sp):
            def load(to, what, signal):
                sp.dma_start(to, what).then_inc(signal, 16)

            load(wk_sb, wkT, wk_loaded)
            load(ctx_t[:, 0, :], ctxT[:, 0, :], ctx_loaded[0])
            load(bk_sb[:, :], bk, bk_loaded)
            load(x_t[:, 0, :, :], xT[0], xt_loaded[0])
            load(x_in[:, 0, :, :], x_pairs[0], x_loaded[0])
            load(ctx_t[:, 1, :], ctxT[:, 1, :], ctx_loaded[1])
            load(gates_in[:, :], gates.partition_broadcast(P), gates_loaded)
            load(gamma_b, gamma.partition_broadcast(P), gamma_beta_loaded)
            load(beta_b, beta.partition_broadcast(P), gamma_beta_loaded)
            for i in range(SHARED_CHUNKS // 2):
                if i > 1:
                    load(ctx_t[:, i, :], ctxT[:, i, :], ctx_loaded[i])
                    load(x_t[:, i - 1, :, :], xT[i - 1], xt_loaded[i - 1])
                load(stage_s[:, 2 * i:2 * i + 2, :], wsrc[2 * i:2 * i + 2].rearrange("c p n -> p c n"), shared_loaded[i])
            load(router_w[:, :, :], gwT, router_loaded)
            load(x_in[:, 1, :, :], x_pairs[1], x_loaded[1])
            load(x_t[:, 3, :, :], xT[3], xt_loaded[3])
            sp.wait_ge(fill_ready, 1)
            sp.dma_start(meta_d.rearrange("(p c) k -> p (c k)", p=P),
                         fill.rearrange("p c k -> p (c k)")).then_inc(cleared, 16)
            sp.dma_start(hid_d[T:T + P, :], zero.bitcast(fp16)).then_inc(cleared, 16)
            sp.dma_start(out[T:T + P, :], zero).then_inc(cleared, 16)

            def store_x1(n):
                for t in range(2):
                    sp.wait_ge(x1_ready, 2 * n + t + 1)
                    sp.dma_start(x1_tiles[ds(2 * n + t, 1)].rearrange("a p d -> p (a d)"), x1_buf[:, t, :])\
                      .then_inc(x1_stored[t], 16)

            def store_tokens(n):
                for t in range(2):
                    sp.wait_ge(tokens_low, 2 * n + t + 1)
                    sp.dma_start(hid_tiles[ds(2 * n + t, 1)].rearrange("a p d -> p (a d)"),
                                 halves[t].rearrange("p s d -> p (s d)")).then_inc(tokens_stored[t], 16)

            def load_x1(m, t):
                if not (isinstance(m, int) and m == 0):
                    sp.wait_ge(out_stored[t], 16 * m)
                    sp.sem_inc(sp_held, 1)
                sp.wait_ge(x1_stored[t], 16 * (m + 1))
                sp.dma_start(rows[:, t, :], x1_tiles[ds(2 * m + t, 1)].rearrange("a p d -> p (a d)"))\
                  .then_inc(x1_loaded[t], 16)

            def store_out(m, t):
                sp.wait_ge(rows_ready, 2 * m + t + 1)
                sp.dma_start(out_tiles[ds(2 * m + t, 1)].rearrange("a p d -> p (a d)"), rows[:, t, :])\
                  .then_inc(out_stored[t], 16)

            def step(n, r):
                if not (isinstance(n, int) and n == NPAIR - 1):
                    sp.wait_ge(tokens_low, 2 * n)
                    sp.dma_start(x_in[:, 1 - r, :, :], x_pairs[ds(n + 1, 1)].rearrange("a p t d -> p (a t) d"))\
                      .then_inc(x_loaded[1 - r], 16)
                load_x1(n - 1, 0)
                if not (isinstance(n, int) and n == 1):
                    store_out(n - 2, 1)
                load_x1(n - 1, 1)
                store_x1(n)
                store_tokens(n)
                store_out(n - 1, 0)

            def load_meta(s, r):
                if not (isinstance(s, int) and s < 2):
                    sp.wait_ge(meta_loaded[r], 16 * (s // 2) if isinstance(s, int) else 8 * (s - r))
                row = sp.value_load(tile_row[0:1, ds(s, 1)], min_val=0, max_val=META_ROWS - P)
                sp.dma_start(meta[:, ds(s, 1), :].rearrange("p a k -> p (a k)"), meta_d[ds(row, P), :])\
                  .then_inc(meta_loaded[r], 16)

            store_x1(0)
            store_tokens(0)
            pair_steps(sp, step)
            load_x1(NPAIR - 1, 0)
            store_out(NPAIR - 2, 1)
            load_x1(NPAIR - 1, 1)
            sp.wait_ge(tables_ready, 1)
            sp.wait_ge(slots_scattered, 64 * NPAIR)
            load_meta(0, 0)
            load_meta(1, 1)
            store_out(NPAIR - 1, 0)
            with sp.Fori(1, TABLE // 2) as k:
                load_meta(2 * k, 0)
                load_meta(2 * k + 1, 1)
            if TABLE % 2:
                load_meta(TABLE - 1, 0)
            sp.wait_ge(out_stored[0], 16 * NPAIR)
            sp.wait_ge(out_stored[1], 16 * NPAIR)
            sp.wait_ge(rows_added, 16 * SLOT_TILES)

        @block.gpsimd
        def _(pool):
            pool.memset(id32, 0.0).then_inc(pool_order, 1)
            pool.memset(id16[:, :], 0.0).then_inc(pool_order, 1)
            pool.memset(ones[:, :], 1.0).then_inc(pool_order, 1)
            pool.wait_ge(pool_order, 3)
            for m in (id32, id16[:, :]):
                pool.affine_select(out=m, in_=m, compare_op=ALU.not_equal, fill=1.0, base=0,
                                   pattern=[[-1, P]], channel_multiplier=1).then_inc(constants_made, 1)
            pool.affine_select(out=below[:, :], in_=ones[:, :], compare_op=ALU.is_gt, fill=0.0, base=0,
                               pattern=[[1, P]], channel_multiplier=-1).then_inc(constants_made, 1)
            pool.memset(half_m[:, :], -0.5).then_inc(constants_made, 1)
            pool.memset(act_hl[:, :, :, F:FP], 0.0).then_inc(constants_made, 1)
            pool.memset(before[:, :, :], 0.0).then_inc(constants_made, 1)
            pool.iota(top8_at[:, :, :], [[0, 2], [1, 8]], base=0, channel_multiplier=0).then_inc(constants_made, 1)
            pool.iota(slot_of[:, :, :], [[0, 2], [P, 2]], base=0, channel_multiplier=1).then_inc(constants_made, 1)
            pool.iota(tile_expert[:, :], [[1, TABLE]], base=0, channel_multiplier=0).then_inc(constants_made, 1)
            pool.iota(filla, [[1, META_ROWS // P]], base=0, channel_multiplier=META_ROWS // P).then_inc(constants_made, 1)
            pool.memset(fill, 0).then_inc(constants_made, 1)
            pool.wait_ge(constants_made, 11)

            def quarter_low_half(n, u):
                pool.wait_ge(quarter_high, 4 * (n - 1) + u + 1)
                w = wr[:, ds(n - 1, 1), :, :].rearrange("p a s n -> p (a s) n")
                c = slice(u * CHUNK, (u + 1) * CHUNK)
                pool.tensor_tensor(w[:, 1, c], stage[:, u % 2, :], w[:, 0, c], ALU.subtract).then_inc(quarter_low, 1)

            def hidden_low_half(U, p):
                pool.wait_ge(hidden_high, U + 1)
                pool.tensor_tensor(act_hl[:, p, 1, 0:F], act_h[:, p, :], act_hl[:, p, 0, 0:F], ALU.subtract)\
                    .then_inc(hidden_low, 1)

            def root_sims(n):
                pool.wait_ge(sims_var_ready, n + 1)
                pool.tensor_tensor(sims_r[:, :], sims_q[:, :], half_m[:, :], ALU.pow).then_inc(sims_root, 1)

            def root_x1(n):
                pool.wait_ge(x1_var_ready, n + 1)
                pool.tensor_tensor(x1_r[:, :], x1_q[:, :], half_m[:, :], ALU.pow).then_inc(x1_root, 1)

            def tokens_low_half(n, r):
                for t in range(2):
                    pool.wait_ge(tokens_high, 2 * n + t + 1)
                    pool.tensor_tensor(halves[t][:, 1, :], x_in[:, r, t, :], halves[t][:, 0, :], ALU.subtract)\
                        .then_inc(tokens_low, 1)

            def scatter(m, t):
                pool.wait_ge(slots_ready, m + 1)
                pool.sem_inc(pool_held, 1)
                for c in range(2):
                    pool.indirect_dma_start(
                        out=meta_d, out_offset=bass.IndirectOffsetOnAxis(slot_of[:, c, t:t + 1], 0),
                        in_=slot_entry[:, t, c, :], in_offset=None).then_inc(slots_scattered, 16)

            def first_step():
                hidden_low_half(0, 0)
                root_sims(1)
                quarter_low_half(1, 0)
                hidden_low_half(1, 1)
                quarter_low_half(1, 1)
                root_x1(1)
                quarter_low_half(1, 2)
                hidden_low_half(2, 0)
                tokens_low_half(1, 1)
                quarter_low_half(1, 3)

            def step(n, r):
                if isinstance(n, int) and n == 1:
                    first_step()
                    return
                U = first_unit(n)
                hidden_low_half(U, 1)
                root_sims(n)
                if isinstance(n, int) and n == 2:
                    pool.wait_ge(cleared, 48)
                scatter(n - 2, 0)
                quarter_low_half(n, 0)
                hidden_low_half(U + 1, 0)
                scatter(n - 2, 1)
                quarter_low_half(n, 1)
                hidden_low_half(U + 2, 1)
                root_x1(n)
                quarter_low_half(n, 2)
                hidden_low_half(U + 3, 0)
                tokens_low_half(n, r)
                quarter_low_half(n, 3)

            root_sims(0)
            root_x1(0)
            tokens_low_half(0, 0)
            pair_steps(pool, step)

            def gather(s, r):
                pool.wait_ge(meta_loaded[r], 16 * (s // 2 + 1) if isinstance(s, int) else 8 * (s - r) + 16)
                if not (isinstance(s, int) and s < 2):
                    pool.wait_ge(tokens_transposed, NTILE + s - 1)
                pool.tensor_copy(gather_rows[:, r:r + 1], meta[:, ds(s, 1), 0:1].rearrange("p a k -> p (a k)"))\
                    .then_inc(gather_rows_ready, 1)
                pool.wait_ge(gather_rows_ready, s + 1)
                pool.sem_inc(pool_held, 1)
                pool.indirect_dma_start(
                    out=gathered[:, r, :, :].rearrange("p s d -> p (s d)"), out_offset=None, in_=hid_d,
                    in_offset=bass.IndirectOffsetOnAxis(gather_rows[:, r:r + 1], 0)).then_inc(slots_gathered[r], 16)

            U = first_unit(NPAIR)
            hidden_low_half(U, 1)
            scatter(NPAIR - 2, 0)
            scatter(NPAIR - 2, 1)
            hidden_low_half(U + 1, 0)
            scatter(NPAIR - 1, 0)
            scatter(NPAIR - 1, 1)
            hidden_low_half(U + 2, 1)
            hidden_low_half(U + 3, 0)
            pool.wait_ge(up_ready, UNITS_SHARED - 4)
            pool.wait_ge(tokens_stored[0], 16 * NPAIR)
            pool.wait_ge(tokens_stored[1], 16 * NPAIR)
            gather(0, 0)
            hidden_low_half(U + 4, 1)
            gather(1, 1)

            def slot_step(s, r):
                if not (isinstance(s, int) and s == SLOT_TILES):
                    gather(s + 2, r)
                    hidden_low_half(UNITS_SHARED + s, r)
                if not (isinstance(s, int) and s == 0):
                    pool.tensor_copy(add_rows[:, 1 - r:2 - r], meta[:, ds(s - 1, 1), 0:1].rearrange("p a k -> p (a k)"))\
                        .then_inc(add_rows_ready, 1)
                    pool.wait_ge(add_rows_ready, s)
                    pool.wait_ge(rows_ready, NTILE + s)
                    if isinstance(s, int) and s == 1:
                        pool.wait_ge(out_stored[0], 16 * NPAIR)
                        pool.wait_ge(out_stored[1], 16 * NPAIR)
                    else:
                        pool.wait_ge(rows_added, 16 * (s - 1))
                    pool.sem_inc(pool_held, 1)
                    pool.indirect_dma_start(
                        out=out, out_offset=bass.IndirectOffsetOnAxis(add_rows[:, 1 - r:2 - r], 0),
                        in_=rows[:, 1 - r, :], in_offset=None, compute_op=ALU.add).then_inc(rows_added, 16)

            slot_steps(pool, slot_step)

        @block.scalar
        def _(act):
            def prep_kv(b):
                if b == 0:
                    act.wait_ge(bk_loaded, 16)
                act.wait_ge(kv_ready, b + 1)
                act.activation(kv_t[:, b, :], prep_ps[b][:, :], ACT.Identity, bias=bk_sb[:, 0:1],
                               accum_out=ksum[:, b:b + 1]).then_inc(kv_biased, 1)

            def prep_keys(b):
                act.wait_ge(kv_transposed, b + 1)
                if b >= 2:
                    act.wait_ge(xkv_ready, b - 1)
                act.activation(kv_keys[b % 2].rearrange("p c d -> p (c d)"), prep_ps[b][:, :], ACT.Copy)\
                   .then_inc(kv_keys_out, 1)

            def prep_xkv(b):
                act.wait_ge(xkv_ready, b + 1)
                cols = slice(2 * P, I) if b == 0 else slice(0, I)
                act.activation(xkv_t[:, b, cols], prep_ps[b][:, cols], ACT.Copy).then_inc(xkv_out, 1)

            def columns(n, r):
                act.wait_ge(xkv_out, n // 2 + 1 if isinstance(n, int) else B)
                act.wait_ge(sims_ready, 2 * n)
                cols = xkv_t[:, n // 2, :] if isinstance(n, int) else \
                    xkv_t[:, ds((n - r) // 2, 1), :].rearrange("p a i -> p (a i)")
                act.activation(pair_cols.rearrange("p t i -> p (t i)"), cols[:, 2 * P * r:2 * P * (r + 1)],
                               ACT.Copy).then_inc(columns_out, 1)

            def exp_sims(n):
                act.wait_ge(max_ready, n + 1)
                for t in range(2):
                    act.activation(x1_buf[:, t, :], x1_buf[:, t, :], ACT.Exp, bias=neg_max[:, t:t + 1],
                                   accum_out=esum[:, t:t + 1]).then_inc(sims_exp, 1)

            def exp_router(m):
                act.wait_ge(router_max_ready, m + 1)
                for t in range(2):
                    act.activation(top_exp[:, t, :], top8[:, t, :], ACT.Exp, bias=neg_top[:, t:t + 1], scale=1.0 / WSCALE,
                                   accum_out=router_sum[:, t:t + 1]).then_inc(router_exp, 1)

            def norm(n, r):
                act.wait_ge(shift_ready, n + 1)
                for t in range(2):
                    act.activation(x_in[:, r, t, :], x1_buf[:, t, :], ACT.Identity, bias=x1_shift[:, t:t + 1],
                                   scale=x1_r[:, t:t + 1]).then_inc(tokens_normed, 1)
                    act.wait_ge(tokens_normed, 2 * n + t + 1)
                    if not (isinstance(n, int) and n == 0):
                        act.wait_ge(tokens_transposed, 2 * n - 1 + t)
                        act.wait_ge(tokens_stored[t], 16 * n)
                    act.activation(halves[t][:, 0, :], x_in[:, r, t, :], ACT.Copy).then_inc(tokens_high, 1)

            def shared_high(c):
                act.wait_ge(shared_loaded[c // 2], 16)
                act.activation(ws[:, c // QUARTERS, 0, (c % QUARTERS) * CHUNK:(c % QUARTERS + 1) * CHUNK],
                               stage_s[:, c, :], ACT.Copy, scale=WSCALE).then_inc(shared_high_made, 1)

            def split_quarter(n, u):
                c = 4 * (n - 1) + u
                act.wait_ge(quarter_loaded[u % 2], 16 * (2 * (n - 1) + u // 2 + 1))
                if u == 0 and isinstance(n, int):
                    if n == 2:
                        act.wait_ge(shared_low_made, SHARED_CHUNKS)
                    if n == NPAIR - 1:
                        act.wait_ge(sims_ready, 2 * NPAIR)
                        act.wait_ge(columns_out, NPAIR)
                        act.wait_ge(tokens_low, 2 * (NPAIR - 1))
                    if n == NPAIR:
                        act.wait_ge(tokens_transposed, NTILE)
                        act.wait_ge(tokens_low, NTILE)
                        act.wait_ge(tokens_stored[0], 16 * NPAIR)
                        for t in range(2):
                            act.wait_ge(x1_stored[t], 16 * NPAIR)
                w = wr[:, ds(n - 1, 1), :, :].rearrange("p a s n -> p (a s) n")
                high = w[:, 0, u * CHUNK:(u + 1) * CHUNK]
                last = isinstance(n, int) and n == NPAIR
                if not last:
                    act.activation(stage[:, u % 2, :], stage[:, u % 2, :], ACT.Copy, scale=WSCALE)\
                       .then_inc(quarter_scaled, 1)
                if not (isinstance(n, int) and c in (0, EXPERT_CHUNKS - 1)):
                    if last and u > 0:
                        act.wait_ge(last_low_made, u)
                    else:
                        act.wait_ge(quarter_low, c)
                    act.dma_start(stage[:, (u + 1) % 2, :],
                                  wsrc[ds(SHARED_CHUNKS + c + 1, 1)].rearrange("a p n -> p (a n)"))\
                       .then_inc(quarter_loaded[(u + 1) % 2], 16)
                if last:
                    act.activation(high, stage[:, u % 2, :], ACT.Copy, scale=WSCALE).then_inc(quarter_high, 1)
                else:
                    act.wait_ge(quarter_scaled, c + 1)
                    act.activation(high, stage[:, u % 2, :], ACT.Copy).then_inc(quarter_high, 1)

            def mlp_tanh(U, p):
                act.wait_ge(gate_ready, U + 1)
                act.activation(act_h[:, p, :], g_ps[:, 0:F], ACT.Tanh, scale=0.5 / WSCALE).then_inc(tanh_ready, 1)

            def mlp_high(U, p):
                act.wait_ge(hidden_ready, U + 1)
                act.activation(act_hl[:, p, 0, 0:F], act_h[:, p, :], ACT.Copy).then_inc(hidden_high, 1)

            def mlp_act(U, p):
                mlp_tanh(U, p)
                mlp_high(U, p)

            def first_step():
                mlp_act(0, 0)
                prep_xkv(3)
                split_quarter(1, 0)
                mlp_tanh(1, 1)
                exp_sims(1)
                mlp_high(1, 1)
                columns(2, 0)
                split_quarter(1, 1)
                exp_router(0)
                mlp_tanh(2, 0)
                split_quarter(1, 2)
                mlp_high(2, 0)
                norm(1, 1)
                split_quarter(1, 3)

            def step(n, r):
                if isinstance(n, int) and n == 1:
                    first_step()
                    return
                U = first_unit(n)
                mlp_act(U, 1)
                split_quarter(n, 0)
                mlp_act(U + 1, 0)
                exp_sims(n)
                if not (isinstance(n, int) and n == NPAIR - 1):
                    columns(n + 1, 1 - r)
                mlp_tanh(U + 2, 1)
                split_quarter(n, 1)
                mlp_high(U + 2, 1)
                exp_router(n - 1)
                split_quarter(n, 2)
                mlp_act(U + 3, 0)
                norm(n, r)
                split_quarter(n, 3)

            act.wait_ge(constants_made, 11)
            act.activation(table[:, :], half_m[:, :], ACT.Tanh)
            prep_kv(0)
            prep_keys(0)
            act.wait_ge(gates_loaded, 16)
            act.activation(gates_t[:, :], gates_in[:, :], ACT.Tanh).then_inc(gates_tanh, 1)
            act.wait_ge(first_xkv_ready, 1)
            act.activation(pair_cols.rearrange("p t i -> p (t i)"), d_ps[:, 0:2 * P], ACT.Copy).then_inc(columns_out, 1)
            prep_kv(1)
            prep_xkv(0)
            shared_high(0)
            prep_keys(1)
            prep_kv(2)
            shared_high(1)
            exp_sims(0)
            columns(1, 1)
            prep_keys(2)
            prep_xkv(1)
            for c in range(2, 5):
                shared_high(c)
            norm(0, 0)
            prep_xkv(2)
            prep_kv(3)
            shared_high(5)
            prep_keys(3)
            shared_high(6)
            shared_high(7)
            for c in range(2):
                act.dma_start(stage[:, c, :], wsrc[SHARED_CHUNKS + c]).then_inc(quarter_loaded[c], 16)
            pair_steps(act, step)
            U = first_unit(NPAIR)
            mlp_act(U, 1)
            split_quarter(NPAIR, 0)
            mlp_tanh(U + 1, 0)
            exp_router(NPAIR - 1)
            mlp_high(U + 1, 0)
            split_quarter(NPAIR, 1)
            mlp_act(U + 2, 1)
            split_quarter(NPAIR, 2)
            mlp_act(U + 3, 0)
            split_quarter(NPAIR, 3)
            mlp_act(U + 4, 1)

            def slot_step(s, r):
                if not (isinstance(s, int) and s == SLOT_TILES):
                    mlp_act(UNITS_SHARED + s, r)
                if isinstance(s, int) and s == 0:
                    act.wait_ge(rows_ready, NTILE)
                    act.dma_start(out_tiles[NTILE - 1], rows[:, 1, :]).then_inc(out_stored[1], 16)

            slot_steps(act, slot_step)

        @block.vector
        def _(dve):
            chain = {"base": 0, "n": 0}

            def tick(ins):
                chain["n"] += 1
                ins.then_inc(vector_order, 1)

            def settle():
                dve.wait_ge(vector_order, chain["base"] + chain["n"])

            def held():
                dve.sem_inc(dve_held, 1)

            dve.memset(zero, 0.0).then_inc(vector_order, 1)
            chain["n"] += 1
            dve.wait_ge(constants_made, 11)
            tick(dve.tensor_copy(iota8[:, :, :], top8_at[:, :, :]))
            tick(dve.tensor_copy(token_id[:, :], slot_of[:, 0, :]))
            tick(dve.tensor_copy(iota_s[:, :], tile_expert[:, :]))
            tick(dve.tensor_scalar(filla, filla, P - 1, None, ALU.bitwise_and))
            settle()
            tick(dve.tensor_scalar(first_slot[:, :, :], iota8[:, :, :], float(T), None, ALU.mult))
            dve.tensor_scalar(fill[:, :, 0], filla, float(T), None, ALU.add).then_inc(fill_ready, 1)

            def center(b):
                dve.wait_ge(kv_biased, b + 1)
                tick(dve.tensor_scalar(kmean[:, b:b + 1], ksum[:, b:b + 1], -1.0 / I, None, ALU.mult))
                settle()
                dve.tensor_scalar(kv_t[:, b, :], kv_t[:, b, :], kmean[:, b:b + 1], None, ALU.add).then_inc(kv_centred, 1)

            def router_weights():
                dve.wait_ge(router_loaded, 16)
                tick(dve.tensor_scalar(router_hl[:, 0, :, :], router_w[:, :, :], WSCALE, None, ALU.mult))
                settle()
                dve.scalar_tensor_tensor(router_hl[:, 1, :, :].rearrange("p c e -> p (c e)"),
                                         router_w[:, :, :].rearrange("p c e -> p (c e)"), WSCALE,
                                         router_hl[:, 0, :, :].rearrange("p c e -> p (c e)"),
                                         ALU.mult, ALU.subtract).then_inc(router_split, 1)

            def shared_low(c):
                dve.wait_ge(shared_high_made, c + 1)
                w = ws[:, c // QUARTERS, :, (c % QUARTERS) * CHUNK:(c % QUARTERS + 1) * CHUNK]
                dve.scalar_tensor_tensor(w[:, 1, :], stage_s[:, c, :], WSCALE, w[:, 0, :],
                                         ALU.mult, ALU.subtract).then_inc(shared_low_made, 1)

            def last_low(u):
                dve.wait_ge(quarter_high, EXPERT_CHUNKS - QUARTERS + u + 1)
                w = wr[:, E - 1, :, u * CHUNK:(u + 1) * CHUNK]
                dve.scalar_tensor_tensor(w[:, 1, :], stage[:, u % 2, :], WSCALE, w[:, 0, :],
                                         ALU.mult, ALU.subtract).then_inc(last_low_made, 1)

            def mlp_hidden(U, p):
                dve.wait_ge(tanh_ready, U + 1)
                tick(dve.scalar_tensor_tensor(act_h[:, p, :], act_h[:, p, :], 1.0, g_ps[:, 0:F], ALU.add, ALU.mult))
                settle()
                dve.wait_ge(up_ready, U + 1)
                dve.scalar_tensor_tensor(act_h[:, p, :], act_h[:, p, :], 0.5 / WSCALE ** 2, u_ps[:, 0:F],
                                         ALU.mult, ALU.mult).then_inc(hidden_ready, 1)

            def hidden_out(U, p):
                dve.wait_ge(hidden_transposed, U + 1)
                dve.tensor_copy(act_t[:, p, :, :, :], ht_v).then_inc(hidden_left, 1)

            def shared_out(m, t):
                dve.wait_ge(down_ready, 4 * m + 2 * t + 2)
                dve.wait_ge(x1_loaded[t], 16 * (m + 1))
                dve.scalar_tensor_tensor(rows[:, t, :], d_ps[:, :], ffn_gate[:, 0:1], rows[:, t, :], ALU.mult, ALU.add)\
                   .then_inc(rows_ready, 1)

            def tokens_out(m, t, slot):
                dve.wait_ge(tokens_transposed, 2 * m + t + 1)
                dve.tensor_copy(ring[:, slot, t, :, :, :], xt_ps[:, :, :, :]).then_inc(tokens_left, 1)

            def attention_stats(n, r):
                dve.wait_ge(x_loaded[r], 16 * (n // 2 + 1) if isinstance(n, int) else 8 * (n - r) + 16)
                for t in range(2):
                    tick(dve.bn_stats(stats_x[:, t, :], x_in[:, r, t, :]))
                if isinstance(n, int) and n == 0:
                    center(1)
                for t in range(2):
                    dve.wait_ge(sims_ready, 2 * n + t + 1)
                    tick(dve.bn_stats(stats_sims[:, t, :], sim_ps[:, t, :]))

            def attention_scale():
                settle()
                held()
                for t in range(2):
                    tick(dve.bn_aggr(moments_x[:, t, :], stats_x[:, t, :]))
                    tick(dve.bn_aggr(moments_sims[:, t, :], stats_sims[:, t, :]))
                settle()
                tick(dve.tensor_scalar(x_term[:, :], moments_x[:, :, 1], LN_EPS, SIM_EPS * H, ALU.add, ALU.mult))
                settle()
                dve.tensor_tensor(sims_q[:, :], x_term[:, :], moments_sims[:, :, 1], ALU.add).then_inc(sims_var_ready, 1)

            def attention_logits(n):
                dve.wait_ge(sims_root, n + 1)
                if isinstance(n, int) and n == 0:
                    dve.wait_ge(gamma_beta_loaded, 32)
                for t in range(2):
                    if not (isinstance(n, int) and n == 0):
                        dve.wait_ge(x1_stored[t], 16 * n)
                    dve.scalar_tensor_tensor(x1_buf[:, t, :], sim_ps[:, t, :], sims_r[:, t:t + 1], gamma_b,
                                             ALU.mult, ALU.mult).then_inc(sims_left, 1)

            def attention_top(n):
                for t in range(2):
                    dve.wait_ge(sims_left, 2 * n + t + 1)
                    held()
                    tick(dve.tensor_tensor_reduce(out=x1_buf[:, t, :], in0=x1_buf[:, t, :], in1=beta_b, scale=1.0,
                                                  scalar=-3.0e38, op0=ALU.add, op1=ALU.max,
                                                  accum_out=sims_max[:, t:t + 1]))
                settle()
                dve.tensor_scalar(neg_max[:, :], sims_max[:, :], -1.0, None, ALU.mult).then_inc(max_ready, 1)

            def attention_add(n, r):
                dve.wait_ge(sims_exp, 2 * n + 2)
                tick(dve.reciprocal(rsum[:, :], esum[:, :]))
                settle()
                tick(dve.tensor_scalar(coef[:, :], rsum[:, :], gates_t[:, 0:1], None, ALU.mult))
                settle()
                for t in range(2):
                    dve.scalar_tensor_tensor(x1_buf[:, t, :], x1_buf[:, t, :], coef[:, t:t + 1], x_in[:, r, t, :],
                                             ALU.mult, ALU.add).then_inc(x1_ready, 1)

            def attention_var(n):
                for t in range(2):
                    dve.wait_ge(x1_ready, 2 * n + t + 1)
                    tick(dve.bn_stats(stats_x1[:, t, :], x1_buf[:, t, :]))
                settle()
                held()
                for t in range(2):
                    tick(dve.bn_aggr(moments_x1[:, t, :], stats_x1[:, t, :]))
                settle()
                dve.tensor_scalar(x1_q[:, :], moments_x1[:, :, 1], LN_EPS, None, ALU.add).then_inc(x1_var_ready, 1)

            def attention_norm(n):
                dve.wait_ge(x1_root, n + 1)
                dve.scalar_tensor_tensor(x1_shift[:, :], moments_x1[:, :, 0], -1.0, x1_r[:, :], ALU.mult, ALU.mult)\
                   .then_inc(shift_ready, 1)

            def route_choose(m):
                dve.wait_ge(logits_ready, m + 1)
                dve.tensor_copy(logits[:, :, :].rearrange("p t e -> p (t e)"), logits_ps).then_inc(logits_left, 1)
                dve.wait_ge(logits_left, m + 1)
                held()
                for t in range(2):
                    tick(dve.max(top8[:, t, :], logits[:, t, :]))
                settle()
                held()
                for t in range(2):
                    tick(dve.max_index(top8_at[:, t, :], top8[:, t, :], logits[:, t, :]))
                dve.tensor_scalar(neg_top[:, :], top8[:, :, 0], -1.0 / WSCALE, None, ALU.mult).then_inc(router_max_ready, 1)
                settle()
                tick(dve.tensor_copy(choice[:, :, :], top8_at[:, :, 0:2]))
                settle()
                for c in range(2):
                    tick(dve.tensor_tensor(mask[:, c, :, :], iota8[:, :, :],
                                           choice[:, :, c:c + 1].broadcast_to((P, 2, E)), ALU.is_equal))
                settle()
                tick(dve.tensor_tensor(both[:, :, :], mask[:, 0, :, :], mask[:, 1, :, :], ALU.add))
                settle()
                tick(dve.tensor_tensor(before[:, 1, :], before[:, 0, :], both[:, 0, :], ALU.add))
                settle()
                dve.tensor_tensor(before[:, 2, :], before[:, 1, :], both[:, 1, :], ALU.add).then_inc(counts_ready, 1)

            def route_place(m):
                dve.wait_ge(ranks_ready, m + 1)
                dve.tensor_tensor(ranks[:, :, :].rearrange("p t e -> p (t e)"), ranks_ps,
                                  first_slot[:, :, :].rearrange("p t e -> p (t e)"), ALU.add).then_inc(ranks_left, 1)
                dve.wait_ge(counts_ready, m + 1)
                tick(dve.tensor_copy(before[:, 0, :], before[:, 2, :]))
                dve.wait_ge(router_exp, 2 * m + 2)
                tick(dve.reciprocal(router_rsum[:, :], router_sum[:, :]))
                dve.wait_ge(ranks_left, m + 1)
                for c in range(2):
                    tick(dve.tensor_tensor(chosen_rank[:, c, :, :], mask[:, c, :, :], ranks[:, :, :], ALU.mult))
                settle()
                tick(dve.tensor_reduce(slot_f[:, :, :].rearrange("p c t -> p (c t)"),
                                       chosen_rank[:, :, :, :].rearrange("p c t e -> p (c t) e"), AX.X, ALU.add))
                tick(dve.tensor_tensor(probs[:, :, :], top_exp[:, :, 0:2],
                                       router_rsum[:, :].unsqueeze(2).broadcast_to((P, 2, 2)),
                                       ALU.mult))
                settle()
                if not (isinstance(m, int) and m == 0):
                    dve.wait_ge(slots_scattered, 64 * m)
                tick(dve.tensor_copy(slot_of[:, :, :], slot_f[:, :, :]))
                tick(dve.tensor_reduce(probs_sum[:, :], probs[:, :, :], AX.X, ALU.add))
                settle()
                tick(dve.tensor_scalar(probs_sum_eps[:, :], probs_sum[:, :], 1e-20, None, ALU.add))
                settle()
                tick(dve.reciprocal(probs_rsum[:, :], probs_sum_eps[:, :]))
                settle()
                tick(dve.tensor_tensor(slot_entry[:, :, :, 1].bitcast(fp32), probs[:, :, :],
                                       probs_rsum[:, :].unsqueeze(2).broadcast_to((P, 2, 2)), ALU.mult))
                for t in range(2):
                    tick(dve.tensor_copy(slot_entry[:, t, :, 0], token_id[:, t:t + 1].broadcast_to((P, 2))))
                settle()
                dve.tensor_scalar(token_id[:, :], token_id[:, :], float(2 * P), None, ALU.add).then_inc(slots_ready, 1)

            def slot_tables():
                tick(dve.tensor_scalar(tile_count[:, 0, :], totals_ps[0:1, :], float(P - 1), None, ALU.add))
                settle()
                tick(dve.tensor_scalar(tile_count[:, 1, :], tile_count[:, 0, :], P.bit_length() - 1, None,
                                       ALU.arith_shift_right))
                settle()
                tick(dve.tensor_copy(ends[:, 0, :], tile_count[:, 1, :]))
                settle()
                for i in range(3):
                    d = 1 << i
                    tick(dve.tensor_copy(ends[:, i + 1, 0:d], ends[:, i, 0:d]))
                    tick(dve.tensor_tensor(ends[:, i + 1, d:E], ends[:, i, d:E], ends[:, i, 0:E - d], ALU.add))
                    settle()
                ends_b = ends[:, 3:4, :].broadcast_to((1, TABLE, E))
                tick(dve.tensor_tensor(past, iota_s[:, :].unsqueeze(2).broadcast_to((1, TABLE, E)), ends_b, ALU.is_ge))
                settle()
                tick(dve.tensor_tensor(past_end, past, ends_b, ALU.mult))
                tick(dve.tensor_reduce(tab[:, 0, :], past, AX.X, ALU.add))
                settle()
                tick(dve.tensor_reduce(tab[:, 1, :], past_end, AX.X, ALU.max))
                settle()
                tick(dve.tensor_scalar(tile_expert[:, :], tab[:, 0, :], float(E - 1), None, ALU.min))
                tick(dve.tensor_tensor(tab[:, 2, :], iota_s[:, :], tab[:, 1, :], ALU.subtract))
                settle()
                tick(dve.tensor_scalar(tab[:, 2, :], tab[:, 2, :], float(P), None, ALU.mult))
                settle()
                dve.scalar_tensor_tensor(tile_row[:, :], tab[:, 0, :], float(T), tab[:, 2, :], ALU.mult, ALU.add)\
                   .then_inc(tables_ready, 1)

            def first_step():
                tokens_out(0, 0, 0)
                center(3)
                tokens_out(0, 1, 0)
                for c in range(4, SHARED_CHUNKS):
                    shared_low(c)
                mlp_hidden(0, 0)
                router_weights()
                attention_stats(1, 1)
                attention_scale()
                attention_logits(1)
                hidden_out(0, 0)
                attention_top(1)
                mlp_hidden(1, 1)
                route_choose(0)
                attention_add(1, 1)
                hidden_out(1, 1)
                attention_var(1)
                mlp_hidden(2, 0)
                attention_norm(1)
                route_place(0)
                shared_out(0, 0)

            def step(n, r):
                if isinstance(n, int) and n == 1:
                    first_step()
                    return
                U = first_unit(n)
                attention_stats(n, r)
                hidden_out(U - 1, 0)
                tokens_out(n - 1, 0, 1 - r)
                mlp_hidden(U, 1)
                tokens_out(n - 1, 1, 1 - r)
                attention_scale()
                hidden_out(U, 1)
                mlp_hidden(U + 1, 0)
                attention_logits(n)
                attention_top(n)
                shared_out(n - 2, 1)
                hidden_out(U + 1, 0)
                route_choose(n - 1)
                mlp_hidden(U + 2, 1)
                attention_add(n, r)
                attention_var(n)
                hidden_out(U + 2, 1)
                mlp_hidden(U + 3, 0)
                attention_norm(n)
                route_place(n - 1)
                shared_out(n - 1, 0)

            center(0)
            attention_stats(0, 0)
            attention_scale()
            attention_logits(0)
            attention_top(0)
            center(2)
            shared_low(0)
            dve.wait_ge(gates_tanh, 1)
            tick(dve.tensor_scalar(ffn_gate[:, :], gates_t[:, 1:2], 1.0 / WSCALE, None, ALU.mult))
            attention_add(0, 0)
            attention_var(0)
            shared_low(1)
            attention_norm(0)
            for c in range(2, 4):
                shared_low(c)

            STEP_TICKS = 43
            step(1, 1)
            step(2, 0)
            before_loop = chain["n"]
            with dve.Fori(1, NPAIR // 2 - 1) as k:
                chain["base"], chain["n"] = before_loop + (k - 1) * (2 * STEP_TICKS), 0
                step(2 * k + 1, 1)
                step(2 * k + 2, 0)
                assert chain["n"] == 2 * STEP_TICKS, chain["n"]
            chain["base"], chain["n"] = 0, before_loop + (NPAIR // 2 - 2) * 2 * STEP_TICKS
            step(NPAIR - 1, 1)

            U = first_unit(NPAIR)
            hidden_out(U - 1, 0)
            tokens_out(NPAIR - 1, 0, 1)
            mlp_hidden(U, 1)
            tokens_out(NPAIR - 1, 1, 1)
            hidden_out(U, 1)
            route_choose(NPAIR - 1)
            mlp_hidden(U + 1, 0)
            last_low(0)
            shared_out(NPAIR - 2, 1)
            route_place(NPAIR - 1)
            hidden_out(U + 1, 0)
            mlp_hidden(U + 2, 1)
            last_low(1)
            slot_tables()
            hidden_out(U + 2, 1)
            mlp_hidden(U + 3, 0)
            last_low(2)
            shared_out(NPAIR - 1, 0)
            last_low(3)
            hidden_out(U + 3, 0)
            mlp_hidden(U + 4, 1)

            def slot_tokens_out(s, r):
                dve.wait_ge(tokens_transposed, NTILE + s + 1)
                dve.tensor_copy(slots_t[:, r, :, :, :], xt_ps[:, :, :, :]).then_inc(tokens_left, 1)

            def slot_step(s, r):
                U = UNITS_SHARED + s
                hidden_out(U - 1, 1 - r)
                if not (isinstance(s, int) and s == SLOT_TILES):
                    slot_tokens_out(s + 1, 1 - r)
                    mlp_hidden(U, r)
                if isinstance(s, int) and s == 0:
                    shared_out(NPAIR - 1, 1)
                    return
                dve.wait_ge(down_ready, U)
                if isinstance(s, int) and s < 3:
                    dve.wait_ge(out_stored[s - 1], 16 * NPAIR)
                else:
                    dve.wait_ge(rows_added, 16 * (s - 2))
                w = meta[:, ds(s - 1, 1), 1:2].rearrange("p a k -> p (a k)").bitcast(fp32)
                dve.tensor_scalar(rows[:, 1 - r, :], d_ps[:, :], w, ffn_gate[:, 0:1], ALU.mult, ALU.mult)\
                   .then_inc(rows_ready, 1)

            slot_tokens_out(0, 0)
            head = chain["n"]
            for s in range(3):
                slot_step(s, s % 2)
            assert chain["n"] == head + 3
            with dve.Fori(1, SLOT_TILES // 2) as k:
                chain["base"], chain["n"] = head + 3 + (k - 1) * 2, 0
                slot_step(2 * k + 1, 1)
                slot_step(2 * k + 2, 0)
            chain["base"], chain["n"] = 0, head + 3 + (SLOT_TILES // 2 - 1) * 2
            slot_step(SLOT_TILES, 1)

        @block.tensor
        def _(pe):
            PRODUCTS = ((0, 0), (0, 1), (1, 0))
            UP_FIRST = 1

            def prep_kv(b):
                pe.wait_ge(ctx_loaded[b], 16)
                pe.matmul(prep_ps[b][:, :], wk_sb, ctx_t[:, b, :], start=True, stop=True).then_inc(kv_ready, 1)

            def prep_keys(b):
                pe.wait_ge(kv_centred, b + 1)
                for c in range(HC):
                    mm = pe.transpose(prep_ps[b][:, c * P:(c + 1) * P], kv_t[:, b, c * P:(c + 1) * P], id32)
                mm.then_inc(kv_transposed, 1)

            def prep_xkv(b):
                pe.wait_ge(kv_keys_out, b + 1)
                pe.wait_ge(xt_loaded[b], 16)
                cols = slice(2 * P, I) if b == 0 else slice(0, I)
                for c in range(HC):
                    mm = pe.matmul(prep_ps[b][:, cols], kv_keys[b % 2][:, c, :], x_t[:, b, c, cols],
                                   start=(c == 0), stop=(c == HC - 1))
                mm.then_inc(xkv_ready, 1)

            def first_columns():
                pe.wait_ge(kv_keys_out, 1)
                pe.wait_ge(xt_loaded[0], 16)
                for c in range(HC):
                    mm = pe.matmul(d_ps[:, 0:2 * P], kv_keys[0][:, c, :], x_t[:, 0, c, 0:2 * P],
                                   start=(c == 0), stop=(c == HC - 1))
                mm.then_inc(first_xkv_ready, 1)

            def sims(n, r):
                pe.wait_ge(columns_out, n + 1)
                kv = kv_t[:, n // 2, :] if isinstance(n, int) else \
                    kv_t[:, ds((n - r) // 2, 1), :].rearrange("p a i -> p (a i)")
                for t in range(2):
                    if not (isinstance(n, int) and n == 0):
                        pe.wait_ge(sims_left, 2 * n - 1 + t)
                    pe.matmul(sim_ps[:, t, :], pair_cols[:, t, :], kv, start=True, stop=True).then_inc(sims_ready, 1)

            def transpose_tokens(src):
                for h in range(2):
                    for c in range(HC):
                        mm = pe.transpose(xt_ps[:, h, c, :], src[:, h, c * P:(c + 1) * P], id16[:, :])
                mm.then_inc(tokens_transposed, 1)

            def pair_tokens(m, t):
                pe.wait_ge(tokens_low, 2 * m + t + 1)
                if not (isinstance(m, int) and m == 0 and t == 0):
                    pe.wait_ge(tokens_left, 2 * m + t)
                transpose_tokens(halves[t])

            def router_logits(m, slot):
                pe.wait_ge(tokens_left, 2 * m + 2)
                if isinstance(m, int) and m == 0:
                    pe.wait_ge(router_split, 1)
                else:
                    pe.wait_ge(ranks_left, m)
                for t in range(2):
                    for c in range(HC):
                        for i, (a, b) in enumerate(PRODUCTS):
                            mm = pe.matmul(logits_ps[:, t * E:(t + 1) * E], ring[:, slot, t, a, c, :],
                                           router_hl[:, b, c, :],
                                           start=(c == 0 and i == 0), stop=(c == HC - 1 and i == 2))
                mm.then_inc(logits_ready, 1)

            def router_ranks(m):
                pe.wait_ge(counts_ready, m + 1)
                pe.matmul(ranks_ps, below[:, :], both[:, :, :].rearrange("p t e -> p (t e)"), start=True, stop=False)
                mm = pe.matmul(ranks_ps, ones[:, :], before[:, 0:2, :].rearrange("p t e -> p (t e)"),
                               start=False, stop=True)
                if isinstance(m, int) and m == NPAIR - 1:
                    mm = pe.matmul(totals_ps, ones[:, :], before[:, 2, :], start=True, stop=True)
                mm.then_inc(ranks_ready, 1)

            def up_or_gate(ps, at, xs, w, chunks=range(HC)):
                for c in chunks:
                    for i, (a, b) in enumerate(PRODUCTS):
                        mm = pe.matmul(ps[:, 0:F], xs[:, a, c, :], w[:, b, at + c * F:at + (c + 1) * F],
                                       start=(c == 0 and i == 0), stop=(c == HC - 1 and i == 2))
                return mm

            def gate(xs, w):
                up_or_gate(g_ps, GATE, xs, w).then_inc(gate_ready, 1)

            def up_first(xs, w):
                up_or_gate(u_ps, UP, xs, w, range(UP_FIRST))

            def up_rest(xs, w):
                up_or_gate(u_ps, UP, xs, w, range(UP_FIRST, HC)).then_inc(up_ready, 1)

            def transpose_hidden(U, p):
                pe.wait_ge(hidden_low, U + 1)
                for h in range(2):
                    for c in range(FC):
                        mm = pe.transpose(ht_v[:, h, c, :], act_hl[:, p, h, c * P:(c + 1) * P], id16[:, :])
                mm.then_inc(hidden_transposed, 1)

            def down(U, p, w, first, last):
                pe.wait_ge(hidden_left, U + 1)
                for c in range(FC):
                    for i, (a, b) in enumerate(PRODUCTS):
                        mm = pe.matmul(d_ps[:, :], act_t[:, p, a, c, :], w[:, b, DOWN + c * H:DOWN + (c + 1) * H],
                                       start=(first and c == 0 and i == 0), stop=(last and c == FC - 1 and i == 2))
                mm.then_inc(down_ready, 1)

            def unit(n, r, j, between=None, after=None):
                U, p = first_unit(n) + j, (j + 1) % 2
                xs = ring[:, r, 1, :, :, :] if j == 0 else ring[:, 1 - r, j // 3, :, :, :]
                w, w_before = ws[:, p, :, :], ws[:, 1 - p, :, :]
                if j in (1, 3):
                    pe.wait_ge(tokens_left, 2 * (n - 1) + j // 3 + 1)
                if isinstance(n, int) and n == 1 and j < 3:
                    pe.wait_ge(shared_low_made, j * QUARTERS)
                    pe.wait_ge(xkv_out, 3)
                piped = not (isinstance(n, int) and n == 1 and j == 1)
                if piped:
                    pe.wait_ge(hidden_ready, U)
                gate(xs, w)
                up_first(xs, w)
                if piped:
                    transpose_hidden(U - 1, 1 - p)
                if between:
                    between()
                up_rest(xs, w)
                if after:
                    after()
                if piped:
                    if p == 1 and not (isinstance(n, int) and n == 1):
                        pe.wait_ge(rows_ready, 2 * n - 3 + j // 2)
                    if isinstance(n, int) and n == 1 and j == 2:
                        pe.wait_ge(xkv_out, B)
                    down(U - 1, 1 - p, w_before, p == 1, p == 0)

            def first_step():
                pair_tokens(0, 0)
                pair_tokens(0, 1)
                prep_keys(3)
                unit(1, 1, 1)
                prep_xkv(3)
                router_logits(0, 0)
                unit(1, 1, 2)
                unit(1, 1, 3, lambda: router_ranks(0))
                sims(2, 0)

            def step(n, r):
                if isinstance(n, int) and n == 1:
                    first_step()
                    return
                m = n - 1
                unit(n, r, 0, lambda: pair_tokens(m, 0), lambda: pair_tokens(m, 1))
                unit(n, r, 1)
                router_logits(m, 1 - r)
                unit(n, r, 2)
                router_ranks(m)
                unit(n, r, 3)
                if not (isinstance(n, int) and n == NPAIR - 1):
                    sims(n + 1, 1 - r)

            pe.wait_ge(constants_made, 11)
            pe.wait_ge(wk_loaded, 16)
            prep_kv(0)
            prep_keys(0)
            first_columns()
            prep_kv(1)
            sims(0, 0)
            prep_xkv(0)
            prep_kv(2)
            prep_keys(1)
            prep_xkv(1)
            prep_keys(2)
            sims(1, 1)
            prep_xkv(2)
            prep_kv(3)
            pair_steps(pe, step)

            def expert(s):
                e = pe.value_load(tile_expert[0:1, ds(s, 1)], min_val=0, max_val=E - 1)
                return wr[:, ds(e, 1), :, :].rearrange("p a s n -> p (a s) n")

            def slot_tokens(s, r):
                pe.wait_ge(slots_gathered[r], 16 * (s // 2 + 1) if isinstance(s, int) else 8 * (s - r) + 16)
                pe.wait_ge(tokens_left, NTILE + s)
                transpose_tokens(gathered[:, r, :, :])

            unit(NPAIR, 0, 0, lambda: pair_tokens(NPAIR - 1, 0), lambda: pair_tokens(NPAIR - 1, 1))
            router_logits(NPAIR - 1, 1)
            unit(NPAIR, 0, 1)
            router_ranks(NPAIR - 1)
            unit(NPAIR, 0, 2)
            unit(NPAIR, 0, 3)
            unit(NPAIR + 1, 1, 0, None, lambda: slot_tokens(0, 0))
            pe.wait_ge(tables_ready, 1)
            pe.wait_ge(quarter_low, EXPERT_CHUNKS - QUARTERS)
            pe.wait_ge(last_low_made, QUARTERS)

            def slot_step(s, r):
                U = UNITS_SHARED + s
                last, first = isinstance(s, int) and s == SLOT_TILES, isinstance(s, int) and s == 0
                if not last:
                    w = expert(s)
                    pe.wait_ge(tokens_left, NTILE + s + 1)
                    pe.wait_ge(hidden_ready, U)
                    gate(slots_t[:, r, :, :, :], w)
                    up_first(slots_t[:, r, :, :, :], w)
                transpose_hidden(U - 1, 1 - r)
                if not last:
                    slot_tokens(s + 1, 1 - r)
                    up_rest(slots_t[:, r, :, :, :], w)
                if first:
                    down(U - 1, 1, ws[:, 1, :, :], False, True)
                else:
                    w = expert(s - 1)
                    pe.wait_ge(rows_ready, NTILE + s - 1)
                    down(U - 1, 1 - r, w, True, True)

            slot_steps(pe, slot_step)


_OUTS = [((T + P, H), "float32")]


def kernel(**inputs):
    import numpy as np
    import concourse.bacc as bacc
    from concourse.bass_utils import run_bass_kernel_spmd

    a = {k: np.asarray(v) for k, v in inputs.items()}

    def unit(gate, up, down):
        parts = [m.T.reshape(HC, P, F).transpose(1, 0, 2).reshape(P, HC * F) for m in (gate, up)]
        d = np.zeros((FP, H), down.dtype)
        d[0:F] = down.T
        parts.append(d.reshape(FC, P, H).transpose(1, 0, 2).reshape(P, FC * H))
        return np.concatenate(parts, axis=1)

    sg, su, sd = a["L0_ffn_sw_gate"], a["L0_ffn_sw_up"], a["L0_ffn_sw_down"]
    units = [unit(sg[i * F:(i + 1) * F], su[i * F:(i + 1) * F], sd[:, i * F:(i + 1) * F]) for i in range(SHARED_UNITS)]
    units += [unit(a["L0_ffn_w_gate"][e], a["L0_ffn_w_up"][e], a["L0_ffn_w_down"][e]) for e in range(E)]
    wsrc = np.stack(units).reshape(SHARED_UNITS + E, P, QUARTERS, CHUNK).transpose(0, 2, 1, 3).reshape(NCHUNK, P, CHUNK)
    arrays = {
        "x": a["x"].reshape(T, H),
        "xT": a["x"].transpose(0, 2, 1).reshape(B, HC, P, I).transpose(0, 2, 1, 3),
        "ctxT": a["ctx_512"].transpose(2, 0, 1),
        "wkT": a["L0_xattn_W_k"].T,
        "bk": a["L0_xattn_b_k"].reshape(DC, 1),
        "gates": np.concatenate([a["g_xattn"], a["g_ffn"]]),
        "gamma": a["L0_xattn_ln_gamma"],
        "beta": a["L0_xattn_ln_beta"],
        "gwT": a["L0_ffn_gate_weight"].T.reshape(HC, P, E).transpose(1, 0, 2),
        "wsrc": wsrc,
    }
    nc = bacc.Bacc("TRN2", target_bir_lowering=False, num_devices=1)
    args = []
    for name in arrays:
        arrays[name] = np.ascontiguousarray(arrays[name])
        args.append(nc.dram_tensor(name, arrays[name].shape, mybir.dt.from_np(arrays[name].dtype),
                                   kind="ExternalInput").ap())
    shape, dtype = _OUTS[0]
    args.append(nc.dram_tensor("out", shape, mybir.dt.from_np(np.dtype(dtype)), kind="ExternalOutput").ap())
    flamingo_block(nc, *args)
    r = run_bass_kernel_spmd(nc, [arrays], core_ids=[0])
    return r.results[0]["out"][0:T].reshape(B, I, H)
```
